# Optimizing a Trainium2 kernel written in Bass

```python
import numpy as np
import jax
import jax.numpy as jnp

def _softmax(x, axis=-1):
    return jax.nn.softmax(x, axis=axis)

def _gelu(x):
    return jax.nn.gelu(x, approximate=True)

def _silu(x):
    return jax.nn.silu(x)

def _sigmoid(x):
    return jax.nn.sigmoid(x)

def _layernorm(x, axis=-1, eps=1e-05):
    m = jnp.mean(x, axis=axis, keepdims=True)
    v = jnp.var(x, axis=axis, keepdims=True)
    return (x - m) / jnp.sqrt(v + eps)

def _scatter_add(tgt, idx, src, axis=0):
    return tgt.at[idx].add(src)

def _segment_sum(src, seg, n):
    return jax.ops.segment_sum(src, seg, n)
kernel_name = 'mk_adj_resnorm_d4_adj_r2_37f6c3'

def setup_inputs(seed: int=0):
    np.random.seed(seed)
    _w = jnp.asarray

    def _rec_inputs():
        import jax
        import jax.numpy as jnp
        _gk = jax.random.key(seed)
        x = -0.003407 + 1.001 * jax.random.normal(jax.random.fold_in(_gk, 1), (3327, 128), jnp.float32)
        _a = jax.random.bernoulli(jax.random.fold_in(_gk, 2), 0.00961827, (3327, 3327))
        _a = jnp.logical_or(_a, jnp.swapaxes(_a, -1, -2))
        _a = jnp.logical_or(_a, jnp.eye(3327, dtype=bool))
        _af = _a.astype(jnp.float32)
        _af = _af * jax.random.uniform(jax.random.fold_in(_gk, 3), (3327, 3327), jnp.float32, 0.05, 5.06092)
        adj = _af
        return (x, adj)
    x, adj = _rec_inputs()

    def _L0_gnn_setup():
        import jax, jax.numpy as jnp
        import numpy as np
        N = 512
        D = 128
        H = 8
        key = jax.random.key(seed)
        ks = jax.random.split(key, 7)
        s = (D * H) ** (-0.5)
        return {'x': jax.random.normal(ks[0], (N, D), dtype=jnp.float32), 'spatial_encoding': jax.random.normal(ks[1], (N, N), dtype=jnp.float32), 'edge_encoding': jax.random.normal(ks[2], (N, N), dtype=jnp.float32), 'Wq': jax.random.normal(ks[3], (D * H, D), dtype=jnp.float32) * s, 'Wk': jax.random.normal(ks[4], (D * H, D), dtype=jnp.float32) * s, 'Wv': jax.random.normal(ks[5], (D * H, D), dtype=jnp.float32) * s, 'Wo': jax.random.normal(ks[6], (D, D * H), dtype=jnp.float32) * s}
    _L0_gnn_all = _L0_gnn_setup()
    _L0_gnn_in = {k: v for k, v in _L0_gnn_all.items() if k in ('Wq', 'Wk', 'Wv', 'Wo')}
    del _L0_gnn_all

    def _L1_gnn_setup():
        import jax, jax.numpy as jnp
        import numpy as np
        NEG = -9000000000000000.0
        ALPHA = 0.2
        key = jax.random.key(seed)
        k1, k2, k3, k4, k5 = jax.random.split(key, 5)
        N, F_in, F_out = (4096, 128, 128)
        x = jax.random.normal(k1, (N, F_in), dtype=jnp.float32)
        adj = jax.random.randint(k2, (N, N), 0, 2).astype(jnp.float32)
        W = jax.random.normal(k3, (F_in, F_out), dtype=jnp.float32) * (1.0 / np.sqrt(F_in))
        a1 = jax.random.normal(k4, (F_out,), dtype=jnp.float32) * (1.0 / np.sqrt(2 * F_out))
        a2 = jax.random.normal(k5, (F_out,), dtype=jnp.float32) * (1.0 / np.sqrt(2 * F_out))
        a_bias = jnp.zeros((1,), dtype=jnp.float32)
        return {'x': x, 'adj': adj, 'W': W, 'a1': a1, 'a2': a2, 'a_bias': a_bias}
    _L1_gnn_all = _L1_gnn_setup()
    _L1_gnn_in = {k: v for k, v in _L1_gnn_all.items() if k in ('W', 'a1', 'a2', 'a_bias')}
    del _L1_gnn_all

    def _L2_gnn_setup():
        import jax, jax.numpy as jnp
        import numpy as np
        N, C_IN, C_OUT = (4096, 128, 128)
        BN_EPS = 1e-05
        EDGE_PROB = 0.004
        key = jax.random.key(seed)
        k1, k2, k3, k4, k5, k6 = jax.random.split(key, 6)
        node_features = jax.random.normal(k1, (N, C_IN), dtype=jnp.float32)
        adjacency_matrix = (jax.random.uniform(k2, (N, N)) < EDGE_PROB).astype(jnp.float32)
        s = 1.0 / np.sqrt(C_IN)
        W_n = jax.random.uniform(k3, (C_OUT, C_IN), jnp.float32, -s, s)
        b_n = jax.random.uniform(k4, (C_OUT,), jnp.float32, -s, s)
        W_c = jax.random.uniform(k5, (C_OUT, C_IN), jnp.float32, -s, s)
        b_c = jax.random.uniform(k6, (C_OUT,), jnp.float32, -s, s)
        gamma = jnp.ones((C_OUT,), jnp.float32)
        beta = jnp.zeros((C_OUT,), jnp.float32)
        return {'node_features': node_features, 'adjacency_matrix': adjacency_matrix, 'W_n': W_n, 'b_n': b_n, 'W_c': W_c, 'b_c': b_c, 'gamma': gamma, 'beta': beta}
    _L2_gnn_all = _L2_gnn_setup()
    _L2_gnn_in = {k: v for k, v in _L2_gnn_all.items() if k in ('W_n', 'b_n', 'W_c', 'b_c', 'gamma', 'beta')}
    del _L2_gnn_all

    def _L3_gnn_setup():
        import jax, jax.numpy as jnp
        import numpy as np
        N = 8192
        F_IN = 128
        F_OUT = 128
        key = jax.random.key(seed)
        k1, k2, k3, k4 = jax.random.split(key, 4)
        x = jax.random.normal(k1, (N, F_IN), dtype=jnp.float32)
        adj = jax.random.uniform(k2, (N, N), dtype=jnp.float32)
        bound = 1.0 / np.sqrt(2 * F_IN)
        W = jax.random.uniform(k3, (F_OUT, 2 * F_IN), minval=-bound, maxval=bound, dtype=jnp.float32)
        b = jax.random.uniform(k4, (F_OUT,), minval=-bound, maxval=bound, dtype=jnp.float32)
        return {'x': x, 'adj': adj, 'W': W, 'b': b}
    _L3_gnn_all = _L3_gnn_setup()
    _L3_gnn_in = {k: v for k, v in _L3_gnn_all.items() if k in ('W', 'b')}
    del _L3_gnn_all
    return {'x': x, 'adj': adj, 'L0_gnn_Wq': _L0_gnn_in['Wq'], 'L0_gnn_Wk': _L0_gnn_in['Wk'], 'L0_gnn_Wv': _L0_gnn_in['Wv'], 'L0_gnn_Wo': _L0_gnn_in['Wo'], 'L1_gnn_W': _L1_gnn_in['W'], 'L1_gnn_a1': _L1_gnn_in['a1'], 'L1_gnn_a2': _L1_gnn_in['a2'], 'L1_gnn_a_bias': _L1_gnn_in['a_bias'], 'L2_gnn_W_n': _L2_gnn_in['W_n'], 'L2_gnn_b_n': _L2_gnn_in['b_n'], 'L2_gnn_W_c': _L2_gnn_in['W_c'], 'L2_gnn_b_c': _L2_gnn_in['b_c'], 'L2_gnn_gamma': _L2_gnn_in['gamma'], 'L2_gnn_beta': _L2_gnn_in['beta'], 'L3_gnn_W': _L3_gnn_in['W'], 'L3_gnn_b': _L3_gnn_in['b']}

def reference(x, adj, L0_gnn_Wq, L0_gnn_Wk, L0_gnn_Wv, L0_gnn_Wo, L1_gnn_W, L1_gnn_a1, L1_gnn_a2, L1_gnn_a_bias, L2_gnn_W_n, L2_gnn_b_n, L2_gnn_W_c, L2_gnn_b_c, L2_gnn_gamma, L2_gnn_beta, L3_gnn_W, L3_gnn_b):
    import jax
    import jax.numpy as jnp

    def _L0_gnn_ref(x, spatial_encoding, edge_encoding, Wq, Wk, Wv, Wo):
        import jax, jax.numpy as jnp
        import numpy as np
        N = 512
        D = 128
        H = 8
        n, d = x.shape
        h = Wq.shape[0] // d
        scale = d ** (-0.5)
        q = (x @ Wq.T).reshape(d, n, h)
        k = (x @ Wk.T).reshape(d, n, h)
        v = (x @ Wv.T).reshape(d, n, h)
        a = jnp.einsum('dnh,dmh->dnm', q, k) * scale
        a = a + spatial_encoding + edge_encoding
        a = jax.nn.softmax(a, axis=2)
        out = jnp.einsum('dnm,dmh->dnh', a, v)
        out = out.reshape(n, h * d)
        return out @ Wo.T

    def _L1_gnn_ref(x, adj, W, a1, a2, a_bias):
        import jax, jax.numpy as jnp
        import numpy as np
        NEG = -9000000000000000.0
        ALPHA = 0.2
        h = x @ W
        s1 = h @ a1
        s2 = h @ a2
        e = jax.nn.leaky_relu(s1[:, None] + s2[None, :] + a_bias[0], negative_slope=ALPHA)
        e = jnp.where(adj > 0, e, NEG)
        attention = jax.nn.softmax(e, axis=1)
        return attention @ h

    def _L2_gnn_ref(node_features, adjacency_matrix, W_n, b_n, W_c, b_c, gamma, beta):
        import jax, jax.numpy as jnp
        import numpy as np
        N, C_IN, C_OUT = (4096, 128, 128)
        BN_EPS = 1e-05
        EDGE_PROB = 0.004
        deg = adjacency_matrix.sum(axis=1, keepdims=True)
        deg = jnp.where(deg == 0, jnp.ones_like(deg), deg)
        agg = adjacency_matrix.T @ node_features / deg
        h = agg @ W_n.T + b_n + node_features @ W_c.T + b_c
        mu = h.mean(axis=0)
        var = ((h - mu) ** 2).mean(axis=0)
        h_norm = (h - mu) * jax.lax.rsqrt(var + BN_EPS)
        return jax.nn.relu(gamma * h_norm + beta)

    def _L3_gnn_ref(x, adj, W, b):
        import jax, jax.numpy as jnp
        import numpy as np
        N = 8192
        F_IN = 128
        F_OUT = 128
        neigh = adj @ x
        W_self = W[:, :F_IN]
        W_neigh = W[:, F_IN:]
        return x @ W_self.T + neigh @ W_neigh.T + b
    x = _layernorm(x + _L0_gnn_ref(x, adj, adj, L0_gnn_Wq, L0_gnn_Wk, L0_gnn_Wv, L0_gnn_Wo), axis=-1)
    x = _layernorm(x + _L1_gnn_ref(x, adj, L1_gnn_W, L1_gnn_a1, L1_gnn_a2, L1_gnn_a_bias), axis=-1)
    x = _layernorm(x + _L2_gnn_ref(x, adj, L2_gnn_W_n, L2_gnn_b_n, L2_gnn_W_c, L2_gnn_b_c, L2_gnn_gamma, L2_gnn_beta), axis=-1)
    x = _layernorm(x + _L3_gnn_ref(x, adj, L3_gnn_W, L3_gnn_b), axis=-1)
    return x

_drawn_inputs = setup_inputs


def setup_inputs(seed=0):
    import zlib

    import numpy as np

    out = dict(_drawn_inputs(seed))
    spreads = {'L2_gnn_gamma': (1.0, 0.2), 'L2_gnn_beta': (0.0, 0.1)}
    factors = {'L0_gnn_Wq': 8.0, 'L0_gnn_Wk': 8.0, 'L2_gnn_b_n': 8.0, 'L2_gnn_b_c': 8.0, 'L3_gnn_b': 8.0}
    for name, (base, spread) in spreads.items():
        noise = np.random.default_rng([zlib.crc32(name.encode()), seed]).standard_normal(out[name].shape)
        drawn = base * np.exp(spread * noise) if base else spread * noise
        out[name] = jnp.asarray(drawn.astype(out[name].dtype))
    for name, factor in factors.items():
        out[name] = (out[name] * factor).astype(out[name].dtype)
    return out
```

```python
def build(nc, t, out):
    import numpy as np
    import concourse.bass as bass
    from concourse import mybir
    from contextlib import ExitStack

    fp32, bf16, i32 = mybir.dt.float32, mybir.dt.bfloat16, mybir.dt.int32
    ALU, ACT, AX = mybir.AluOpType, mybir.ActivationFunctionType, mybir.AxisListType

    P = 128
    N = 3327
    NT = 26
    NP = NT * P
    HEADS = 128
    F = 8
    TOK = NP * P
    SCALE = float(P) ** -0.5
    EPS = 1e-5

    NBLK = 4
    QB = NP // NBLK
    HALF = QB // 2
    QUART = QB // 4
    BT = NT // 2
    POOL_TILES = (1, 5, 10, 14, 18, 22)
    DVE_TILES = tuple(k for k in range(NT) if k not in POOL_TILES)
    RING = 13
    PAIR = 2 * NT
    PAIRS = HEADS // 2
    LAG_DVE, LAG_POOL = 5, 6
    HEADROOM = 40.0
    SPAN = 120.0

    is_pool = lambda x: x % NT in POOL_TILES
    npool, ndve = 2 * len(POOL_TILES), 2 * len(DVE_TILES)
    pool_no = lambda x: (x // NT) * len(POOL_TILES) + POOL_TILES.index(x % NT)
    dve_no = lambda x: (x // NT) * len(DVE_TILES) + DVE_TILES.index(x % NT)
    av_key = lambda x: x + (LAG_POOL if is_pool(x) else LAG_DVE)
    av_order = sorted(range(PAIR), key=av_key)
    av_no = {x: n for n, x in enumerate(av_order)}

    ctx = ExitStack()
    with ctx:
        sb = lambda name, shape, dt=fp32: ctx.enter_context(nc.sbuf_tensor(name, shape, dt))
        sem = lambda name: ctx.enter_context(nc.semaphore(name))
        dram = lambda name, shape, dt: nc.dram_tensor(name, shape, dt, kind="Internal").ap()

        q_rows = dram("q_rows", (27, TOK), bf16)
        k_rows = dram("k_rows", (24, TOK), bf16)
        v_tok = dram("v_tok", (TOK, F + 1), fp32)
        o_rows = dram("o_rows", (F + 1, TOK), fp32)

        arena = sb("arena", [P, 12 * NP])
        big = lambda n: arena[:, n * NP:(n + 1) * NP]
        ident = sb("ident", [P, P])
        ones = sb("ones", [P, P])
        mean_w = sb("mean_w", [P, P])
        wo = sb("wo", [P, F, P])
        small = sb("small", [P, 64])
        recip_d = sb("recip_d", [P, 2, P])
        zeros = sb("zeros", [1, 512])
        flag = sb("flag", [1, 1], i32)

        slab = arena[:, 0:NT * QB].rearrange("p (k c) -> p k c", k=NT)
        ring = arena[:, NT * QB:(NT + RING) * QB].rearrange("p (k c) -> p k c", k=RING)
        kst = [sb(f"kst{j}", [P, NP], bf16) for j in range(2)]
        qst = [sb(f"qst{j}", [P, QB], bf16) for j in range(2)]
        vst = [sb(f"vst{j}", [P, NT * (F + 1)]) for j in range(2)]
        osb = [sb(f"osb{j}", [P, QUART]) for j in range(2)]

        at = [0]

        def piece(words):
            at[0] += words
            return arena[:, at[0] - words:at[0]]
        wqkv = [piece(F * P) for _ in range(3)]
        xblk = [piece(P) for _ in range(2)]
        parts = [[piece(3 * F * P // 2).bitcast(bf16).rearrange("p (a j) -> p a j", j=P) for _ in range(2)]
                 for _ in range(2)]
        resid = [piece(F * P) for _ in range(2)]
        square = [piece(F * P) for _ in range(2)]
        vtile = [piece(P * (F + 1)) for _ in range(2)]
        adj_s = [piece(NP) for _ in range(2)]
        q_norms, k_norms = piece(NP), piece(NP)
        rest = piece(NP)
        shift_parts = piece(3 * NP // 2).bitcast(bf16).rearrange("p (a c) -> p a c", a=3)
        assert at[0] <= 12 * NP
        stats = small[:, 0:3]
        gmax = small[:, 4:5]
        diag3 = small[:, 8:11]
        gstat = small[:, 12:15]
        roots = small[:, 16:18]
        neg_k, offset, crit, eps_t = (small[:, 20 + n:21 + n] for n in range(4))
        a_max = small[:, 32:32 + NT]

        g_adj, g_prob, g_prob_t = big(0), big(1), big(2)
        g_top, g_neg_max = small[:, 60:61], small[:, 61:62]

        oblk = [big(1)[:, 0:(F + 1) * P], big(2)[:, 0:(F + 1) * P]]
        yblk = [big(3)[:, j * F * P:(j + 1) * F * P] for j in range(2)]
        x_cur = big(0)

        CH = NP // 8
        HN = NP // 2
        chunks = lambda ap: ap.rearrange("p (c n) -> p c n", n=CH)
        ln_d, ln_s = big(1), big(2)
        h_t, h_nat = big(1), big(2)
        a_row, b_row = big(3), big(4)
        x_nat = big(3)
        recip_deg, none_row = big(5), big(6)
        tile_buf = [big(7), big(8)]
        work = [big(9), big(10), big(11)]
        s2_row = big(11)
        wmat = sb("wmat", [P, 5, P])
        vecs = sb("vecs", [P, 8])
        a1_all, a2_all = (sb(f"a{n}_all", [P, P]) for n in (1, 2))
        sel = sb("sel", [P, 4, P])
        stat_k = [sb(f"stat_k{j}", [P, P]) for j in range(2)]
        s2_pair = sb("s2_pair", [P, NT, 2])
        s2_now = [sb(f"s2_now{j}", [P, 2]) for j in range(2)]
        u_nat, deg_nat = sb("u_nat", [P, NT]), sb("deg_nat", [P, NT])
        u_now, zero_col = sb("u_now", [P, 2]), sb("zero_col", [P, 1])
        deg_now = [sb(f"deg_now{j}", [P, 1]) for j in range(2)]
        den_sb = sb("den_sb", [P, CH])
        cols = sb("cols", [P, 16])
        s2_min, u_off, h_sum, bn_bias, bn_mean, bn_var, bn_std, bn_gain = (cols[:, n:n + 1] for n in range(8))
        pool_tick = sb("pool_tick", [P, 4])
        psum = ctx.enter_context(nc.psum_tensor("psum", [P, 8, 512], fp32))
        ps_w = [psum[:, 2 * w:2 * w + 2, :] for w in range(3)]
        s_dve = [psum[:, 2 * b:2 * b + 2, 0:HALF] for b in range(2)]
        s_pool = psum[:, 4:6, 0:HALF]
        acc = [psum[:, 6 + j, 0:QUART] for j in range(2)]

        consts_in = sem("consts_in")
        setup = sem("setup")
        x_in = [sem(f"x_in{j}") for j in range(2)]
        adj_in = [sem(f"adj_in{j}") for j in range(2)]
        proj_done = [sem(f"proj_done{w}") for w in range(3)]
        part1 = [sem(f"part1_{w}") for w in range(2)]
        part2 = [sem(f"part2_{w}") for w in range(2)]
        part3 = [sem(f"part3_{w}") for w in range(2)]
        resid_done = [sem(f"resid_done{w}") for w in range(2)]
        square_free = [sem(f"square_free{w}") for w in range(2)]
        v_ready = sem("v_ready")
        adj_free = sem("adj_free")
        parts_out = [[sem(f"parts_out{w}{j}") for j in range(2)] for w in range(2)]
        v_out = [sem(f"v_out{j}") for j in range(2)]
        stats_ready = sem("stats_ready")
        stats_turned = sem("stats_turned")
        diag_ready = sem("diag_ready")
        stats_spread = sem("stats_spread")
        gstat_ready = sem("gstat_ready")
        roots_ready = sem("roots_ready")
        shift_ready = sem("shift_ready")
        dve_done = sem("dve_done")
        rows_out = sem("rows_out")
        psum_free = [*resid_done, v_ready]

        slab_in = sem("slab_in")
        head_in = [sem(f"head_in{j}") for j in range(2)]
        scores_dve = sem("scores_dve")
        scores_pool = sem("scores_pool")
        biased = sem("biased")
        exp_dve = sem("exp_dve")
        exp_pool = sem("exp_pool")
        bias_multiplied = sem("bias_multiplied")
        values_added = sem("values_added")
        acc_copied = sem("acc_copied")
        head_out = [sem(f"head_out{j}") for j in range(2)]
        attention_out = sem("attention_out")

        flag_ready = sem("flag_ready")
        g_adj_in, g_in, g_scores, g_step, g_max, g_exp = (
            sem(n) for n in ("g_adj_in", "g_in", "g_scores", "g_step", "g_max", "g_exp"))
        g_turned, g_prob_copied, g_summed, g_out_ready, g_stored = (
            sem(n) for n in ("g_turned", "g_prob_copied", "g_summed", "g_out_ready", "g_stored"))
        recip_made = sem("recip_made")
        o_in = [sem(f"o_in{j}") for j in range(2)]
        y_ready = sem("y_ready")
        y_turned = sem("y_turned")
        yt_copied = sem("yt_copied")
        wo_done = sem("wo_done")
        x_row = sem("x_row")
        yt_free = sem("yt_free")
        x_in2 = sem("x_in2")
        final_out = sem("final_out")
        ln_mean, ln_centered, ln_squared, ln_var, ln_std, ln_out = (
            sem(n) for n in ("ln_mean", "ln_centered", "ln_squared", "ln_var", "ln_std", "ln_out"))
        x_ready = sem("x_ready")
        h_made, h_copied = sem("h_made"), sem("h_copied")
        s_made, s1_copied, s2_copied = sem("s_made"), sem("s1_copied"), sem("s2_copied")
        nat_made, nat_copied = sem("nat_made"), sem("nat_copied")
        s2_col_made = sem("s2_col_made")
        tile_in = [sem(f"tile_in{j}") for j in range(2)]
        u_done, deg_done, deg_kept = sem("u_done"), sem("deg_done"), sem("deg_kept")
        u_step = sem("u_step")
        spread_in, spread_out = sem("spread_in"), sem("spread_out")
        mask_ready, mask_used = sem("mask_ready"), sem("mask_used")
        half_in = [sem(f"half_in{j}") for j in range(2)]
        exponent_ready, weights_ready, gat_added = sem("exponent_ready"), sem("weights_ready"), sem("gat_added")
        gat_step = sem("gat_step")
        den_made, den_copied, den_spread, half_done = (
            sem(n) for n in ("den_made", "den_copied", "den_spread", "half_done"))
        stat_ready, sweep_added, sweep_done = sem("stat_ready"), sem("sweep_added"), sem("sweep_done")
        sweep_in = [sem(f"sweep_in{j}") for j in range(2)]
        sum_copied, dense_made, dense_copied = sem("sum_copied"), sem("dense_made"), sem("dense_copied")
        bn_centered, bn_squared, bn_ready, bn_out = (
            sem(n) for n in ("bn_centered", "bn_squared", "bn_ready", "bn_out"))

        block = ctx.enter_context(nc.Block())

        def rows_of(parts_dram, r0, nrows, rb):
            return parts_dram[r0:r0 + nrows, bass.ds(rb * (P * P), P * P)].rearrange("a (r j) -> r a j", j=P)

        def slot_free(eng, nb, p, x, first):
            y = x - RING
            if y >= 0 or not first:
                n = av_no[y] if y >= 0 else av_no[y + PAIR] - PAIR
                eng.wait_ge(values_added, nb * (PAIRS * PAIR) + p * PAIR + n + 1)

        @block.sync
        def _(sp):
            for w, name in enumerate(("Wq", "Wk", "Wv")):
                sp.dma_start(wqkv[w], t[name]).then_inc(consts_in, 16)
            sp.dma_start(wo[:], t["Wo"]).then_inc(consts_in, 16)
            sp.dma_start(wmat[:], t["mats"]).then_inc(consts_in, 16)
            sp.dma_start(vecs[:], t["vecs"]).then_inc(consts_in, 16)
            sp.wait_ge(setup, 12)
            sp.dma_start(o_rows[:, TOK - P:TOK], ones[0:F + 1, :]).then_inc(rows_out, 16)
            with sp.Fori(0, NT // 2) as g:
                for j in range(2):
                    sp.wait_ge(proj_done[2], g * 2 + j + 1)
                    sp.dma_start(xblk[j], t["xT"][:, bass.ds((g * 2 + j) * P, P)]).then_inc(x_in[j], 16)
                    sp.wait_ge(adj_free, g * 2 + j + 1)
                    sp.dma_start(adj_s[j], t["adjN"][bass.ds((g * 2 + j) * P, P), :]).then_inc(adj_in[j], 16)
                    if j == 1:
                        for jj in range(2):
                            rb = g * 2 + jj
                            for w in range(2):
                                sp.wait_ge(part3[w], rb + 2)
                                sp.dma_start(rows_of((q_rows, k_rows)[w], 0, 24, rb), parts[w][jj][:])\
                                    .then_inc(parts_out[w][jj], 16)
                            sp.wait_ge(v_ready, rb + 2)
                            sp.dma_start(v_tok[bass.ds(rb * (P * P), P * P), :]
                                         .rearrange("(r j) f -> r (j f)", j=P), vtile[jj]).then_inc(v_out[jj], 16)
            sp.wait_ge(shift_ready, 1)
            for a in range(3):
                sp.dma_start(q_rows[24 + a, :].rearrange("(b r j) -> r b j", r=P, j=P),
                             shift_parts[:, a, :].rearrange("p (b j) -> p b j", j=P)).then_inc(rows_out, 16)
            sp.wait_ge(rows_out, 64)
            for w in range(2):
                for j in range(2):
                    sp.wait_ge(parts_out[w][j], 16 * (NT // 2 + 1))
            for j in range(2):
                sp.wait_ge(v_out[j], 16 * (NT // 2 + 1))

            def load_keys(key0, j, loaded):
                for r in range(3):
                    sp.dma_start(kst[j][8 * r:8 * r + 8, :], k_rows[0:8, bass.ds(key0, NP)]).then_inc(loaded, 16)
                for r in range(2):
                    sp.dma_start(kst[j][27 + 8 * r:35 + 8 * r, :], k_rows[8:16, bass.ds(key0, NP)])\
                        .then_inc(loaded, 16)
                sp.dma_start(kst[j][43:51, :], k_rows[16:24, bass.ds(key0, NP)]).then_inc(loaded, 16)

            def load_values(key0, j, loaded):
                W = BT * (F + 1)
                v = v_tok[bass.ds(key0, NP), :].rearrange("(s p b) f -> s p (b f)", s=2, p=P)
                sp.dma_start(vst[j][:, 0:W], v[0]).then_inc(loaded, 16)
                sp.dma_start(vst[j][0:P - 1, W:2 * W], v[1, 0:P - 1]).then_inc(loaded, 16)
                sp.dma_start(vst[j][P - 1:P, W:2 * W - (F + 1)], v[1, P - 1:P, 0:W - (F + 1)]).then_inc(loaded, 16)

            def load_head(col0, h, j):
                q0 = h * N + col0
                load_keys(h * N, j, head_in[j])
                sp.dma_start(qst[j][0:27, :], q_rows[0:27, bass.ds(q0, QB)]).then_inc(head_in[j], 16)
                sp.dma_start(qst[j][27:43, :], q_rows[0:16, bass.ds(q0, QB)]).then_inc(head_in[j], 16)
                sp.dma_start(qst[j][43:51, :], q_rows[0:8, bass.ds(q0, QB)]).then_inc(head_in[j], 16)
                load_values(h * N, j, head_in[j])

            def store_head(col0, h, j):
                o0 = h * N + col0
                for c in range(4):
                    sp.dma_start(o_rows[:, bass.ds(o0 + c * QUART, QUART)], osb[j][32 * c:32 * c + F + 1, :])\
                        .then_inc(head_out[j], 16)

            sp.wait_ge(flag_ready, 1)
            narrow = sp.value_load(flag[0:1, 0:1], min_val=0, max_val=1)
            with sp.If(narrow == 1):
                for j in range(2):
                    sp.nop().then_inc(head_out[j], 16)
                with sp.Fori(0, NBLK) as nb:
                    col0 = nb * (-QB) + (NBLK - 1) * QB
                    for j in range(2):
                        sp.wait_ge(head_out[j], nb * (PAIRS * 4 * 16) + 16)
                    for s in range(2):
                        sp.dma_start(slab[:, s * BT:(s + 1) * BT, :],
                                     t["adjT"][s * BT * P:(s + 1) * BT * P, bass.ds(col0, QB)]
                                     .rearrange("(p b) c -> p b c", p=P)).then_inc(slab_in, 16)
                    load_head(col0, 0, 0)
                    load_head(col0, 1, 1)
                    done = nb * (PAIRS * PAIR)
                    heads = nb * HEADS
                    with sp.Fori(0, PAIRS - 1) as p:
                        for j in range(2):
                            sp.wait_ge(values_added, done + p * PAIR + (j + 1) * NT)
                            load_head(col0, (p + 1) * 2 + j, j)
                            sp.wait_ge(acc_copied, heads + p * 2 + j + 1)
                            store_head(col0, p * 2 + j, j)
                    for j in range(2):
                        sp.wait_ge(acc_copied, heads + HEADS - 1 + j)
                        store_head(col0, HEADS - 2 + j, j)

                for j in range(2):
                    sp.wait_ge(head_out[j], NBLK * (PAIRS * 4 * 16) + 16)
            with sp.Else():
                sp.nop().then_inc(g_stored, 16)
                with sp.Fori(0, NT) as i:
                    row0 = i * (-P) + (NT - 1) * P
                    sp.dma_start(g_adj, t["adjN"][bass.ds(row0, P), :]).then_inc(g_adj_in, 16)
                    with sp.Fori(0, HEADS) as h:
                        step = i * HEADS + h
                        sp.wait_ge(g_summed, step + 1)
                        load_keys(h * N, 0, g_in)
                        load_values(h * N, 0, g_in)
                        for r0, rows in ((0, 24), (27, 16), (43, 8)):
                            sp.dma_start(qst[0][r0:r0 + rows, 0:P], q_rows[0:rows, bass.ds(h * N + row0, P)])\
                                .then_inc(g_in, 16)
                        sp.wait_ge(g_out_ready, step + 2)
                        sp.dma_start(o_rows[:, bass.ds((NT - 1) * P + h * N - i * P, P)], osb[0][0:F + 1, 0:P]).then_inc(g_stored, 16)
                sp.wait_ge(g_stored, NT * HEADS * 16 + 16)

            sp.dma_start(x_cur, t["xT"]).then_inc(x_in2, 16)
            with sp.Fori(0, NT // 2) as g:
                for j in range(2):
                    sp.wait_ge(y_turned, g * 2 + j + 1)
                    sp.dma_start(oblk[j].rearrange("p (f j) -> p f j", j=P), rows_of(o_rows, 0, F + 1, g * 2 + j))\
                        .then_inc(o_in[j], 16)
            sp.wait_ge(ln_out, 1)
            with sp.Fori(0, NT // 2) as g:
                for j in range(2):
                    sp.wait_ge(u_done, g * 2 + j + 1)
                    sp.wait_ge(deg_done, g * 2 + j + 1)
                    sp.dma_start(tile_buf[j], t["adjN"][bass.ds((g * 2 + j) * P, P), :]).then_inc(tile_in[j], 16)
            for half in range(2):
                with sp.Fori(0, NT // 2) as g:
                    for j in range(2):
                        sp.wait_ge(mask_ready, half * NT + g * 2 + j + 1)
                        if half == 0:
                            sp.wait_ge(u_done, NT + 2)
                            sp.wait_ge(deg_done, NT + 2)
                        sp.dma_start(tile_buf[j][:, 0:HN], t["adjT"][bass.ds((g * 2 + j) * P, P),
                                                                    half * HN:(half + 1) * HN])\
                            .then_inc(half_in[j], 16)
            for n, name in enumerate(("adjN", "adjT")):
                sp.wait_ge(mask_ready, 2 * NT + 2)
                with sp.Fori(0, NT // 2) as g:
                    for j in range(2):
                        sp.wait_ge(sweep_added, n * NT + g * 2 + j + 1)
                        sp.dma_start(tile_buf[j], t[name][bass.ds((g * 2 + j) * P, P), :]).then_inc(sweep_in[j], 16)
            sp.wait_ge(ln_out, 4)
            sp.dma_start(out, x_cur[:, 0:N]).then_inc(final_out, 16)
            sp.wait_ge(final_out, 16)

        @block.gpsimd
        def _(pool):
            pool.wait_ge(setup, 11)
            nc.gpsimd.affine_select(out=ident[:], in_=ident[:], compare_op=ALU.not_equal, fill=1.0, base=0,
                                    pattern=[[-1, P]], channel_multiplier=1).then_inc(setup, 1)
            pool.wait_ge(flag_ready, 1)
            narrow = pool.value_load(flag[0:1, 0:1], min_val=0, max_val=1)
            with pool.If(narrow == 1):
                with pool.Fori(0, NBLK) as nb:
                    with pool.Fori(0, PAIRS) as p:
                        for x in range(PAIR):
                            if is_pool(x):
                                pool.wait_ge(exp_pool, nb * (PAIRS * npool) + p * npool + pool_no(x) + 1)
                                nc.gpsimd.tensor_tensor(ring[:, x % RING, :], ring[:, x % RING, :], slab[:, x % NT, :],
                                                        ALU.mult).then_inc(bias_multiplied, 1)

            pool.nop().then_inc(mask_ready, 2)
            for half in range(2):
                with pool.Fori(0, NT // 2) as g:
                    for j in range(2):
                        r = half * NT + g * 2 + j
                        pool.wait_ge(mask_used, r + 1)
                        nc.gpsimd.tensor_tensor(pool_tick[:, 2 * j:2 * j + 1], zero_col[:], zero_col[:], ALU.mult)
                        pool.wait_ge(half_in[j], (half * (NT // 2) + g + 1) * 16)
                        nc.gpsimd.tensor_tensor(pool_tick[:, 2 * j + 1:2 * j + 2], zero_col[:], zero_col[:], ALU.mult)
                        nc.gpsimd.tensor_scalar(work[2][:, j * HN:(j + 1) * HN], tile_buf[j][:, 0:HN], 0.0, -1e30,
                                                ALU.is_le, ALU.mult).then_inc(mask_ready, 1)

        @block.tensor
        def _(pe):
            pe.wait_ge(setup, 12)
            pe.wait_ge(consts_in, 96)
            pe.nop().then_inc(proj_done[2], 2)
            with pe.Fori(0, NT // 2) as g:
                for j in range(2):
                    pe.wait_ge(x_in[j], (g + 1) * 16)
                    for w in range(3):
                        pe.wait_ge(psum_free[w], g * 2 + j + 1)
                        for c in range(2):
                            last = nc.tensor.matmul(ps_w[w][:, c, :], xblk[j], wqkv[w][:, c * 512:(c + 1) * 512],
                                                    start=True, stop=True)
                        last.then_inc(proj_done[w], 1)
            pe.wait_ge(stats_ready, 1)
            nc.tensor.transpose(psum[0:3, 0, 0:P], stats, ident[:]).then_inc(stats_turned, 1)
            pe.wait_ge(diag_ready, 1)
            nc.tensor.matmul(psum[:, 1, 0:3], ones[0:3, :], diag3[0:3, :], start=True, stop=True)\
                .then_inc(stats_spread, 1)

            def scores(x, base_dve, base_pool, nb, p, first):
                j, k = divmod(x, NT)
                if k == 0:
                    pe.wait_ge(head_in[j], (nb * PAIRS + p + 1) * (12 * 16))
                s, b = divmod(k, BT)
                keys = kst[j][:, s * BT * P:(s + 1) * BT * P].rearrange("r (p b) -> r b p", b=BT)[:, b, :]
                if is_pool(x):
                    dst, n = s_pool, pool_no(x)
                    if not first or n >= 1:
                        pe.wait_ge(exp_pool, base_pool + n)
                else:
                    n = dve_no(x)
                    dst = s_dve[n % 2]
                    if not first or n >= 2:
                        pe.wait_ge(biased, base_dve + n - 1)
                for c in range(2):
                    last = nc.tensor.matmul(dst[:, c, :], keys, qst[j][:, c * HALF:(c + 1) * HALF],
                                            start=True, stop=True)
                last.then_inc(scores_pool if is_pool(x) else scores_dve, 1)

            def values(x, base_dve, base_pool):
                j, k = divmod(x, NT)
                if is_pool(x):
                    pe.wait_ge(bias_multiplied, base_pool + pool_no(x) + 1)
                else:
                    pe.wait_ge(exp_dve, base_dve + dve_no(x) + 1)
                for c in range(4):
                    last = nc.tensor.matmul(acc[j][32 * c:32 * c + F + 1, :], vst[j][:, k * (F + 1):(k + 1) * (F + 1)],
                                            ring[:, x % RING, c * QUART:(c + 1) * QUART],
                                            start=(k == 0), stop=(av_order[NT - 1 + j * NT] == x))
                last.then_inc(values_added, 1)

            assert all(x // NT == n // NT for n, x in enumerate(av_order))

            def pair(nb, p, first):
                bd, bp = nb * (PAIRS * ndve) + p * ndve, nb * (PAIRS * npool) + p * npool
                for x in range(PAIR):
                    scores(x, bd, bp, nb, p, first)
                    for y in av_order:
                        if not first and x - 1 < av_key(y) - PAIR <= x:
                            values(y, bd - ndve, bp - npool)
                    for y in av_order:
                        if x - 1 < av_key(y) <= x:
                            values(y, bd, bp)

            pe.wait_ge(flag_ready, 1)
            narrow = pe.value_load(flag[0:1, 0:1], min_val=0, max_val=1)
            with pe.If(narrow == 1):
                for j in range(2):
                    nc.tensor.matmul(acc[j], ones[0:1, :], zeros[:, 0:QUART], start=True, stop=True)
                with pe.Fori(0, NBLK) as nb:
                    pair(nb, 0, True)
                    with pe.Fori(1, PAIRS) as p:
                        pair(nb, p, False)
                    for y in av_order:
                        if av_key(y) > PAIR - 1:
                            values(y, nb * (PAIRS * ndve) + (PAIRS - 1) * ndve, nb * (PAIRS * npool) + (PAIRS - 1) * npool)
            with pe.Else():
                pe.nop().then_inc(g_summed, 1)
                with pe.Fori(0, NT) as i:
                    with pe.Fori(0, HEADS) as h:
                        step = i * HEADS + h
                        pe.wait_ge(g_in, (step + 1) * (12 * 16))
                        pe.wait_ge(g_out_ready, step + 1)
                        for c in range(8):
                            last = nc.tensor.matmul(psum[:, c, 0:CH], qst[0][:, 0:P], kst[0][:, c * CH:(c + 1) * CH],
                                                    start=True, stop=True)
                        last.then_inc(g_scores, 1)
                        pe.wait_ge(g_exp, step + 1)
                        for k in range(NT):
                            hs, b = divmod(k, BT)
                            keys = g_prob[:, hs * BT * P:(hs + 1) * BT * P].rearrange("n (p b) -> n b p", b=BT)
                            last = nc.tensor.transpose(psum[:, k // 4, (k % 4) * P:(k % 4 + 1) * P], keys[:, b, :],
                                                       ident[:])
                        last.then_inc(g_turned, 1)
                        pe.wait_ge(g_prob_copied, step + 1)
                        for k in range(NT):
                            last = nc.tensor.matmul(psum[0:F + 1, 7, 0:P], vst[0][:, k * (F + 1):(k + 1) * (F + 1)],
                                                    g_prob_t[:, k * P:(k + 1) * P], start=(k == 0), stop=(k == NT - 1))
                        last.then_inc(g_summed, 1)

            pe.nop().then_inc(y_turned, 2)
            pe.nop().then_inc(wo_done, 2)
            with pe.Fori(0, NT // 2) as g:
                for j in range(2):
                    pe.wait_ge(y_ready, g * 2 + j + 3)
                    pe.wait_ge(yt_copied, g * 2 + j + 1)
                    for f in range(F):
                        last = nc.tensor.transpose(psum[:, f // 4, (f % 4) * P:(f % 4 + 1) * P],
                                                   oblk[j][:, f * P:(f + 1) * P], ident[:])
                    last.then_inc(y_turned, 1)
                    pe.wait_ge(yt_copied, g * 2 + j + 2)
                    pe.wait_ge(x_row, g * 2 + j + 1)
                    for f in range(F):
                        last = nc.tensor.matmul(psum[:, 2 + j, 0:P], wo[:, f, :], yblk[j][:, f * P:(f + 1) * P],
                                                start=(f == 0), stop=(f == F - 1))
                    last.then_inc(wo_done, 1)

            def turned_sums(lhs, rhs, first=True, last=True):
                for c in range(8):
                    out_ = nc.tensor.matmul(psum[:, c, 0:CH], lhs, rhs[:, c * CH:(c + 1) * CH], start=first,
                                            stop=last, skip_group_check=True)
                return out_

            def layernorm(n):
                pe.wait_ge(x_ready, n + 1)
                turned_sums(mean_w[:], x_cur).then_inc(ln_mean, 1)
                pe.wait_ge(ln_squared, n + 1)
                turned_sums(mean_w[:], ln_s).then_inc(ln_var, 1)

            def by_node(src, count):
                for k in range(NT):
                    last = nc.tensor.transpose(psum[:, k // 4, (k % 4) * P:(k % 4 + 1) * P],
                                               src[:, k * P:(k + 1) * P], ident[:])
                last.then_inc(nat_made, 1)

            def zero_banks(n, stop=False):
                for c in range(n):
                    last = nc.tensor.matmul(psum[:, c, 0:CH], ones[0:1, :], zeros[:, 0:CH], start=not stop, stop=stop,
                                            skip_group_check=True)
                return last

            layernorm(0)
            pe.wait_ge(ln_out, 1)
            turned_sums(wmat[:, 0, :], x_cur).then_inc(h_made, 1)
            pe.wait_ge(h_copied, 1)
            turned_sums(a1_all[:], h_t).then_inc(s_made, 1)
            pe.wait_ge(s1_copied, 1)
            turned_sums(a2_all[:], h_t).then_inc(s_made, 1)
            pe.wait_ge(s2_copied, 1)
            for k in range(NT):
                nc.tensor.matmul(psum[:, k // 4, (k % 4) * P:(k % 4 + 1) * P], x_cur[:, k * P:(k + 1) * P],
                                 wmat[:, 0, :], start=True, stop=True)
            for k in range(NT):
                last = nc.tensor.matmul(psum[:, 7, k:k + 1], h_t[:, k * P:(k + 1) * P], vecs[:, 1:2],
                                        start=True, stop=True)
            last.then_inc(nat_made, 1)
            for n in range(2):
                pe.wait_ge(spread_in, n + 1)
                turned_sums(ones[:], work[0]).then_inc(spread_out, 1)
            for half in range(2):
                if half == 0:
                    pe.wait_ge(spread_in, 3)
                else:
                    pe.wait_ge(half_done, half)
                zero_banks(5)
                if half == 0:
                    pe.nop().then_inc(gat_added, 2)
                with pe.Fori(0, NT // 2) as g:
                    for j in range(2):
                        r = half * NT + g * 2 + j
                        pe.wait_ge(weights_ready, r + 1)
                        for c in range(4):
                            nc.tensor.matmul(psum[:, c, 0:CH], stat_k[j][:], work[j][:, c * CH:(c + 1) * CH],
                                             start=False, stop=False, skip_group_check=True)
                        for c in range(4):
                            last = nc.tensor.matmul(psum[32 * c:32 * c + 9, 4, 0:CH], ones[:, 0:9],
                                                    work[j][:, c * CH:(c + 1) * CH], start=False, stop=False,
                                                    skip_group_check=True)
                        last.then_inc(gat_added, 1)
                zero_banks(5, stop=True).then_inc(den_made, 1)
                pe.wait_ge(den_copied, half + 1)
                for c in range(4):
                    last = nc.tensor.matmul(psum[:, 4 + c, 0:CH], sel[:, c, :], den_sb[:], start=True, stop=True)
                last.then_inc(den_spread, 1)
            layernorm(1)
            for n in range(2):
                pe.wait_ge(ln_out, n + 2)
                by_node(x_cur, n)
                pe.wait_ge(nat_copied, n + 2)
                zero_banks(8)
                if n == 0:
                    pe.nop().then_inc(sweep_added, 2)
                with pe.Fori(0, NT // 2) as g:
                    for j in range(2):
                        r = n * NT + g * 2 + j
                        pe.wait_ge(sweep_in[j], (n * (NT // 2) + g + 1) * 16)
                        pe.wait_ge(stat_ready, r + 1)
                        for c in range(8):
                            last = nc.tensor.matmul(psum[:, c, 0:CH], stat_k[j][:],
                                                    tile_buf[j][:, c * CH:(c + 1) * CH],
                                                    start=False, stop=False, skip_group_check=True)
                        last.then_inc(sweep_added, 1)
                zero_banks(8, stop=True).then_inc(sweep_done, 1)
                pe.wait_ge(sum_copied, 2 * n + 1)
                for c in range(8):
                    nc.tensor.matmul(psum[:, c, 0:CH], wmat[:, 1 + 2 * n, :], work[0][:, c * CH:(c + 1) * CH],
                                     start=True, stop=False)
                    last = nc.tensor.matmul(psum[:, c, 0:CH], wmat[:, 2 + 2 * n, :], x_cur[:, c * CH:(c + 1) * CH],
                                            start=False, stop=True)
                last.then_inc(dense_made, 1)
                layernorm(n + 2)

        @block.scalar
        def _(act):
            act.wait_ge(setup, 12)
            act.nop().then_inc(v_ready, 1)
            for j in range(2):
                act.nop().then_inc(parts_out[0][j], 16)
                act.nop().then_inc(parts_out[1][j], 16)
                act.nop().then_inc(v_out[j], 16)
            with act.Fori(0, NT // 2) as g:
                for j in range(2):
                    for w in range(2):
                        act.wait_ge(proj_done[w], g * 2 + j + 1)
                        act.wait_ge(square_free[w], g * 2 + j + 1)
                        nc.scalar.activation(square[w].rearrange("p (b c) -> p b c", b=2), ps_w[w], ACT.Square)
                        act.wait_ge(parts_out[w][j], (g + 1) * 16)
                        nc.scalar.copy(parts[w][j][:, 0:8, :].rearrange("p (b f) c -> p b (f c)", b=2), ps_w[w]).then_inc(part1[w], 1)
                    for w in range(2):
                        act.wait_ge(resid_done[w], g * 2 + j + 2)
                        nc.scalar.copy(parts[w][j][:, 8:16, :].rearrange("p f c -> p (f c)"), resid[w]).then_inc(part2[w], 1)
                    act.wait_ge(proj_done[2], g * 2 + j + 3)
                    act.wait_ge(v_out[j], (g + 1) * 16)
                    for b in range(2):
                        last = nc.scalar.copy(vtile[j].rearrange("p (t f) -> p f t", f=F + 1)[:, 4 * b:4 * b + 4, :],
                                              ps_w[2][:, b, :].rearrange("p (f t) -> p f t", t=P))
                    last.then_inc(v_ready, 1)
            act.wait_ge(gstat_ready, 1)
            nc.scalar.activation(roots, gstat[:, 0:2], ACT.Sqrt).then_inc(roots_ready, 1)
            nc.scalar.activation(q_norms, q_norms, ACT.Sqrt).then_inc(roots_ready, 1)

            def act_pair(nb, p, first):
                bd, bp = nb * (PAIRS * ndve) + p * ndve, nb * (PAIRS * npool) + p * npool
                for x in act_order:
                    if is_pool(x):
                        act.wait_ge(scores_pool, bp + pool_no(x) + 1)
                        slot_free(act, nb, p, x, first)
                        nc.scalar.activation(ring[:, x % RING, :].rearrange("p (u c) -> p u c", u=2), s_pool,
                                             ACT.Exp, scale=SCALE).then_inc(exp_pool, 1)
                    else:
                        act.wait_ge(biased, bd + dve_no(x) + 1)
                        nc.scalar.activation(ring[:, x % RING, :], ring[:, x % RING, :], ACT.Exp,
                                             scale=2.0).then_inc(exp_dve, 1)

            act_order = sorted(range(PAIR), key=lambda x: x + (0.1 if is_pool(x) else 2))
            act.wait_ge(flag_ready, 1)
            narrow = act.value_load(flag[0:1, 0:1], min_val=0, max_val=1)
            with act.If(narrow == 1):
                with act.Fori(0, NBLK) as nb:
                    act.wait_ge(slab_in, (nb + 1) * 32)
                    for k in POOL_TILES:
                        nc.scalar.activation(slab[:, k, :], slab[:, k, :], ACT.Exp, scale=2.0)
                    act_pair(nb, 0, True)
                    with act.Fori(1, PAIRS) as p:
                        act_pair(nb, p, False)
            with act.Else():
                with act.Fori(0, NT) as i:
                    with act.Fori(0, HEADS) as h:
                        step = i * HEADS + h
                        act.wait_ge(g_max, step + 1)
                        nc.scalar.activation(g_prob[:, 0:N], g_prob[:, 0:N], ACT.Exp, bias=g_neg_max).then_inc(g_exp, 1)
                        act.wait_ge(g_turned, step + 1)
                        nc.scalar.copy(g_prob_t[:, 0:24 * P].rearrange("p (b c) -> p b c", c=512), psum[:, 0:6, :])
                        nc.scalar.copy(g_prob_t[:, 24 * P:NP], psum[:, 6, 0:2 * P]).then_inc(g_prob_copied, 1)

            act.nop().then_inc(yt_copied, 1)
            with act.Fori(0, NT // 2) as g:
                for j in range(2):
                    act.wait_ge(y_turned, g * 2 + j + 3)
                    act.wait_ge(wo_done, g * 2 + j + 1)
                    nc.scalar.copy(yblk[j].rearrange("p (b c) -> p b c", b=2), psum[:, 0:2, :]).then_inc(yt_copied, 1)

            all8 = psum[:, :, 0:CH]

            def layernorm(n):
                act.wait_ge(ln_centered, n + 1)
                nc.scalar.activation(ln_s, ln_d, ACT.Square).then_inc(ln_squared, 1)
                act.wait_ge(ln_var, n + 1)
                nc.scalar.activation(chunks(ln_s), all8, ACT.Sqrt, bias=eps_t).then_inc(ln_std, 1)

            def copy_by_node(dst):
                nc.scalar.copy(dst[:, 0:24 * P].rearrange("p (b c) -> p b c", c=512), psum[:, 0:6, :])
                return nc.scalar.copy(dst[:, 24 * P:NP], psum[:, 6, 0:2 * P])

            layernorm(0)
            act.wait_ge(h_made, 1)
            nc.scalar.copy(chunks(h_t), all8).then_inc(h_copied, 1)
            act.wait_ge(s_made, 2)
            nc.scalar.copy(chunks(s2_row), all8).then_inc(s2_copied, 1)
            act.wait_ge(nat_made, 1)
            copy_by_node(h_nat)
            nc.scalar.copy(s2_pair[:, :, 0], psum[:, 7, 0:NT]).then_inc(nat_copied, 1)
            act.nop().then_inc(deg_done, 2)
            with act.Fori(0, NT // 2) as g:
                for j in range(2):
                    act.wait_ge(tile_in[j], (g + 1) * 16)
                    act.wait_ge(deg_kept, g * 2 + j + 1)
                    act.wait_ge(deg_done, g * 2 + j + 2)
                    nc.scalar.activation(work[1], tile_buf[j], ACT.Copy, accum_out=deg_now[j][:])\
                        .then_inc(deg_done, 1)
            for half in range(2):
                with act.Fori(0, NT // 2) as g:
                    for j in range(2):
                        act.wait_ge(exponent_ready, half * NT + g * 2 + j + 1)
                        nc.scalar.activation(work[j][:, 0:HN], work[j][:, 0:HN], ACT.Exp).then_inc(weights_ready, 1)
            layernorm(1)
            act.wait_ge(nat_made, 2)
            copy_by_node(x_nat).then_inc(nat_copied, 1)
            act.wait_ge(dense_made, 1)
            act.wait_ge(sum_copied, 2)
            nc.scalar.activation(chunks(work[1]), all8, ACT.Identity, bias=bn_bias).then_inc(dense_copied, 1)
            act.wait_ge(bn_centered, 1)
            nc.scalar.activation(work[0][:, 0:N], work[2][:, 0:N], ACT.Square, accum_out=bn_var).then_inc(bn_squared, 1)
            act.wait_ge(bn_squared, 1)
            nc.scalar.activation(bn_std, bn_var, ACT.Sqrt, scale=1.0 / N, bias=eps_t).then_inc(bn_squared, 1)
            act.wait_ge(bn_ready, 1)
            nc.scalar.activation(work[0], work[2], ACT.Relu, scale=bn_gain, bias=vecs[:, 6:7]).then_inc(bn_out, 1)
            layernorm(2)
            act.wait_ge(nat_made, 3)
            copy_by_node(x_nat).then_inc(nat_copied, 1)
            act.wait_ge(sweep_done, 2)
            nc.scalar.copy(chunks(work[0]), all8).then_inc(sum_copied, 1)
            layernorm(3)

        @block.vector
        def _(dve):
            done = [0]

            def link(ins):
                done[0] += 1
                ins.then_inc(dve_done, 1)
                dve.wait_ge(dve_done, done[0])

            nc.vector.memset(ones[:], 1.0).then_inc(setup, 1)
            for j in range(2):
                nc.vector.memset(vst[j][:], 0.0).then_inc(setup, 1)
                nc.vector.memset(kst[j][:], 1.0).then_inc(setup, 1)
                nc.vector.memset(qst[j][:], 0.0).then_inc(setup, 1)
                nc.vector.memset(vtile[j], 1.0).then_inc(setup, 1)
            nc.vector.memset(mean_w[:], 1.0 / P)
            nc.vector.memset(zeros[:], 0.0)
            nc.vector.memset(zero_col[:], 0.0)
            nc.vector.memset(eps_t, EPS).then_inc(setup, 1)
            nc.vector.memset(ident[:], 0.0).then_inc(setup, 1)
            for s in (*resid_done, *square_free, *part3):
                dve.nop().then_inc(s, 1)
            dve.nop().then_inc(adj_free, 2)

            dve.wait_ge(consts_in, 96)
            dve.wait_ge(setup, 12)
            nc.vector.tensor_scalar(a1_all[:], ones[:], vecs[:, 0:1], None, ALU.mult)
            nc.vector.tensor_scalar(a2_all[:], ones[:], vecs[:, 1:2], None, ALU.mult)
            for c in range(4):
                nc.vector.tensor_scalar(sel[:, c, :], ones[:], ident[:, 32 * c:32 * c + 1], None, ALU.mult)

            with dve.Fori(0, NT // 2) as g:
                for j in range(2):
                    r = g * 2 + j
                    for w in range(2):
                        dve.wait_ge(part3[w], r + 1)
                        dve.wait_ge(part1[w], r + 1)
                        nc.vector.tensor_tensor(resid[w].rearrange("p (b c) -> p b c", b=2), ps_w[w],
                                                parts[w][j][:, 0:8, :].rearrange("p (b f) c -> p b (f c)", b=2),
                                                ALU.subtract).then_inc(resid_done[w], 1)
                    for w, norms in enumerate((q_norms, k_norms)):
                        nc.vector.tensor_reduce(norms[:, bass.ds(r * P, P)],
                                                square[w].rearrange("p (f t) -> p t f", t=P),
                                                AX.X, ALU.add).then_inc(square_free[w], 1)
                    dve.wait_ge(adj_in[j], (g + 1) * 16)
                    for w in range(2):
                        dve.wait_ge(part2[w], r + 1)
                        nc.vector.tensor_tensor(parts[w][j][:, 16:24, :].rearrange("p f c -> p (f c)"), resid[w],
                                                parts[w][j][:, 8:16, :].rearrange("p f c -> p (f c)"),
                                                ALU.subtract).then_inc(part3[w], 1)
                    nc.vector.tensor_reduce(a_max[:, bass.ds(r, 1)], adj_s[j], AX.X, ALU.max,
                                            apply_absolute_value=True).then_inc(adj_free, 1)

            dve.wait_ge(adj_free, NT + 2)
            dve.wait_ge(square_free[1], NT + 1)
            dve.wait_ge(square_free[0], NT + 1)
            nc.vector.tensor_reduce(stats[:, 0:1], k_norms, AX.X, ALU.max)
            nc.vector.tensor_reduce(stats[:, 1:2], q_norms, AX.X, ALU.max)
            nc.vector.tensor_reduce(stats[:, 2:3], a_max, AX.X, ALU.max).then_inc(stats_ready, 1)
            dve.wait_ge(stats_turned, 1)
            link(nc.vector.tensor_reduce(gmax[0:3, :], psum[0:3, 0, 0:P], AX.X, ALU.max))
            nc.vector.tensor_scalar(diag3[0:3, :], ident[0:3, 0:3], gmax[0:3, :], None, ALU.mult)\
                .then_inc(diag_ready, 1)
            dve.wait_ge(stats_spread, 1)
            nc.vector.tensor_copy(gstat, psum[:, 1, 0:3]).then_inc(gstat_ready, 1)
            dve.wait_ge(gstat_ready, 1)
            link(nc.vector.tensor_scalar(offset, gstat[:, 2:3], -2.0 / SCALE, HEADROOM / SCALE, ALU.mult, ALU.add))
            dve.wait_ge(roots_ready, 2)
            link(nc.vector.tensor_scalar(neg_k, roots[:, 0:1], -1.0, None, ALU.mult))
            link(nc.vector.tensor_scalar(q_norms, q_norms, neg_k, offset, ALU.mult, ALU.add))
            link(nc.vector.tensor_copy(shift_parts[:, 0, :], q_norms))
            link(nc.vector.tensor_tensor(rest, q_norms, shift_parts[:, 0, :], ALU.subtract))
            link(nc.vector.tensor_copy(shift_parts[:, 1, :], rest))
            nc.vector.tensor_tensor(shift_parts[:, 2, :], rest, shift_parts[:, 1, :], ALU.subtract)\
                .then_inc(shift_ready, 1)
            link(nc.vector.tensor_tensor(crit, roots[:, 0:1], roots[:, 1:2], ALU.mult))
            link(nc.vector.tensor_scalar(crit, crit, 2.0 * SCALE, None, ALU.mult))
            link(nc.vector.scalar_tensor_tensor(crit, gstat[:, 2:3], 4.0, crit, ALU.mult, ALU.add))
            nc.vector.tensor_scalar(flag[:], crit[0:1, :], SPAN, None, ALU.is_le).then_inc(flag_ready, 1)

            def copy_sums(nb, p, j, first):
                dve.wait_ge(values_added, nb * (PAIRS * PAIR) + p * PAIR + (j + 1) * NT)
                if not first:
                    dve.wait_ge(head_out[j], nb * (PAIRS * 4 * 16) + p * (4 * 16) + 16)
                nc.vector.tensor_copy(osb[j][:], acc[j]).then_inc(acc_copied, 1)

            def dve_pair(nb, p, first):
                bd = nb * (PAIRS * ndve) + p * ndve
                for x in range(PAIR):
                    if not is_pool(x):
                        dve.wait_ge(scores_dve, bd + dve_no(x) + 1)
                        slot_free(dve, nb, p, x, first)
                        nc.vector.scalar_tensor_tensor(
                            ring[:, x % RING, :].rearrange("p (u c) -> p u c", u=2), s_dve[dve_no(x) % 2], SCALE / 2,
                            slab[:, x % NT, :].rearrange("p (u c) -> p u c", u=2), ALU.mult, ALU.add)\
                            .then_inc(biased, 1)
                    if x == 8 and not first:
                        copy_sums(nb, p - 1, 1, False)
                    if x == NT + 8:
                        copy_sums(nb, p, 0, first)

            dve.wait_ge(flag_ready, 1)
            narrow = dve.value_load(flag[0:1, 0:1], min_val=0, max_val=1)
            with dve.If(narrow == 1):
                with dve.Fori(0, NBLK) as nb:
                    dve.wait_ge(slab_in, (nb + 1) * 32)
                    dve_pair(nb, 0, True)
                    with dve.Fori(1, PAIRS) as p:
                        dve_pair(nb, p, False)
                    copy_sums(nb, PAIRS - 1, 1, False)
            with dve.Else():
                dve.nop().then_inc(g_out_ready, 1)
                with dve.Fori(0, NT) as i:
                    with dve.Fori(0, HEADS) as h:
                        step = i * HEADS + h
                        dve.wait_ge(g_adj_in, (i + 1) * 16)
                        dve.wait_ge(g_scores, step + 1)
                        nc.vector.scalar_tensor_tensor(g_prob.rearrange("p (c n) -> p c n", n=CH), psum[:, :, 0:CH],
                                                       SCALE, g_adj.rearrange("p (c n) -> p c n", n=CH),
                                                       ALU.mult, ALU.add).then_inc(g_step, 1)
                        dve.wait_ge(g_step, step * 4 + 1)
                        nc.vector.tensor_tensor(g_prob, g_prob, g_adj, ALU.add).then_inc(g_step, 1)
                        dve.wait_ge(g_step, step * 4 + 2)
                        nc.vector.tensor_reduce(g_top, g_prob[:, 0:N], AX.X, ALU.max).then_inc(g_step, 1)
                        nc.vector.memset(g_prob[:, N:NP], 0.0).then_inc(g_step, 1)
                        dve.wait_ge(g_step, step * 4 + 4)
                        nc.vector.tensor_scalar(g_neg_max, g_top, -1.0, None, ALU.mult).then_inc(g_max, 1)
                        dve.wait_ge(g_summed, step + 2)
                        dve.wait_ge(g_stored, step * 16 + 16)
                        nc.vector.tensor_copy(osb[0][0:F + 1, 0:P], psum[0:F + 1, 7, 0:P]).then_inc(g_out_ready, 1)

            dve.nop().then_inc(x_row, 2)
            dve.nop().then_inc(y_ready, 2)
            dve.wait_ge(x_in2, 16)
            with dve.Fori(0, NT // 2) as g:
                for j in range(2):
                    r = g * 2 + j
                    dve.wait_ge(o_in[j], (g + 1) * 16)
                    dve.wait_ge(y_ready, r + 1)
                    nc.vector.reciprocal(recip_d[:, j, :], oblk[j][:, F * P:(F + 1) * P]).then_inc(recip_made, 1)
                    dve.wait_ge(recip_made, r + 1)
                    nc.vector.tensor_tensor(oblk[j][:, 0:F * P].rearrange("p (f c) -> p f c", f=F),
                                            oblk[j][:, 0:F * P].rearrange("p (f c) -> p f c", f=F),
                                            recip_d[:, j:j + 1, :].broadcast_to([P, F, P]), ALU.mult)\
                        .then_inc(y_ready, 1)
                    dve.wait_ge(wo_done, r + 3)
                    nc.vector.tensor_tensor(x_cur[:, bass.ds(r * P, P)], psum[:, 2 + j, 0:P],
                                            x_cur[:, bass.ds(r * P, P)], ALU.add).then_inc(x_row, 1)

            all8 = psum[:, :, 0:CH]

            def layernorm(n):
                dve.wait_ge(ln_mean, n + 1)
                nc.vector.tensor_tensor(chunks(ln_d), chunks(x_cur), all8, ALU.subtract).then_inc(ln_centered, 1)
                dve.wait_ge(ln_std, n + 1)
                link(nc.vector.reciprocal(ln_s, ln_s))
                nc.vector.tensor_tensor(x_cur, ln_d, ln_s, ALU.mult).then_inc(ln_out, 1)

            dve.wait_ge(x_row, NT + 2)
            dve.nop().then_inc(x_ready, 1)
            layernorm(0)
            dve.wait_ge(ln_out, 1)
            dve.wait_ge(s_made, 1)
            nc.vector.tensor_scalar(chunks(a_row), all8, vecs[:, 2:3], None, ALU.add).then_inc(s1_copied, 1)
            dve.wait_ge(s2_copied, 1)
            link(nc.vector.tensor_reduce(s2_min, s2_row, AX.X, ALU.min))
            link(nc.vector.tensor_scalar(u_off, s2_min, 1.0, None, ALU.subtract))
            link(nc.vector.tensor_scalar(s2_row, s2_row, u_off, None, ALU.subtract))
            dve.wait_ge(h_copied, 1)
            link(nc.vector.tensor_reduce(h_sum, h_t[:, 0:N], AX.X, ALU.add))
            dve.wait_ge(nat_copied, 1)
            link(nc.vector.tensor_scalar(s2_pair[:, :, 1], s2_pair[:, :, 0], 0.2, None, ALU.mult))
            dve.nop().then_inc(u_done, 2)
            dve.nop().then_inc(deg_kept, 2)
            with dve.Fori(0, NT // 2) as g:
                for j in range(2):
                    r = g * 2 + j
                    dve.wait_ge(tile_in[j], (g + 1) * 16)
                    dve.wait_ge(u_done, r + 2)
                    nc.vector.scalar_tensor_tensor(work[0], tile_buf[j], 0.0, s2_row, ALU.is_gt, ALU.mult)\
                        .then_inc(u_step, 1)
                    dve.wait_ge(u_step, r * 2 + 1)
                    nc.vector.tensor_reduce(u_now[:, j:j + 1], work[0], AX.X, ALU.max).then_inc(u_step, 1)
                    dve.wait_ge(u_step, r * 2 + 2)
                    nc.vector.tensor_tensor(u_nat[:, bass.ds(r, 1)], u_now[:, j:j + 1], zero_col[:], ALU.add)\
                        .then_inc(u_done, 1)
                    dve.wait_ge(deg_done, r + 3)
                    nc.vector.tensor_tensor(deg_nat[:, bass.ds(r, 1)], deg_now[j][:], zero_col[:], ALU.add)\
                        .then_inc(deg_kept, 1)
            dve.wait_ge(deg_kept, NT + 2)
            dve.wait_ge(u_done, NT + 2)
            by_tile = lambda ap: ap.rearrange("p (k c) -> p k c", c=P)
            ident_all = ident[:].rearrange("p (o c) -> p o c", o=1).broadcast_to([P, NT, P])

            def spread(col):
                nc.vector.tensor_tensor(by_tile(work[0]), ident_all,
                                        col[:].rearrange("p (k o) -> p k o", o=1).broadcast_to([P, NT, P]),
                                        ALU.mult).then_inc(spread_in, 1)

            spread(u_nat)
            dve.wait_ge(spread_out, 1)
            nc.vector.tensor_scalar(chunks(none_row), all8, 0.0, None, ALU.is_equal)
            link(nc.vector.scalar_tensor_tensor(chunks(work[1]), all8, u_off, chunks(a_row), ALU.add, ALU.add))
            link(nc.vector.scalar_tensor_tensor(work[2], work[1], 0.2, work[1], ALU.mult, ALU.max))
            link(nc.vector.scalar_tensor_tensor(b_row, a_row, 0.2, work[2], ALU.mult, ALU.subtract))
            link(nc.vector.tensor_tensor(a_row, a_row, work[2], ALU.subtract))
            spread(deg_nat)
            dve.wait_ge(spread_out, 2)
            link(nc.vector.tensor_scalar(chunks(work[1]), all8, 0.0, None, ALU.is_equal))
            link(nc.vector.tensor_tensor(chunks(work[1]), all8, chunks(work[1]), ALU.add))
            link(nc.vector.reciprocal(recip_deg, work[1]))
            dve.nop().then_inc(mask_used, 2)
            dve.nop().then_inc(spread_in, 1)
            for half in range(2):
                cut = slice(half * HN, (half + 1) * HN)
                with dve.Fori(0, NT // 2) as g:
                    for j in range(2):
                        r = half * NT + g * 2 + j
                        k = g * 2 + j
                        low, t_now = work[j][:, HN:2 * HN], work[j][:, 0:HN]
                        dve.wait_ge(gat_added, r + 1)
                        nc.vector.tensor_tensor(stat_k[j][:], h_nat[:, bass.ds(k * P, P)],
                                                h_nat[:, bass.ds(k * P, P)], ALU.max).then_inc(gat_step, 1)
                        dve.wait_ge(mask_used, r + 1)
                        nc.vector.tensor_tensor(s2_now[j][:].rearrange("p (o c) -> p o c", o=1),
                                                s2_pair[:, bass.ds(k, 1), :], s2_pair[:, bass.ds(k, 1), :],
                                                ALU.max).then_inc(gat_step, 1)
                        dve.wait_ge(gat_step, r * 4 + 2)
                        nc.vector.tensor_scalar(low, b_row[:, cut], s2_now[j][:, 1:2], None, ALU.add)\
                            .then_inc(gat_step, 1)
                        dve.wait_ge(gat_step, r * 4 + 3)
                        nc.vector.scalar_tensor_tensor(t_now, a_row[:, cut], s2_now[j][:, 0:1], low,
                                                       ALU.add, ALU.max).then_inc(gat_step, 1)
                        dve.wait_ge(gat_step, r * 4 + 4)
                        dve.wait_ge(mask_ready, r + 3)
                        nc.vector.tensor_tensor(t_now, t_now, work[2][:, j * HN:(j + 1) * HN], ALU.min)\
                            .then_inc(exponent_ready, 1)
                        dve.wait_ge(exponent_ready, r + 1)
                        dve.nop().then_inc(mask_used, 1)
                dve.wait_ge(den_made, half + 1)
                nc.vector.tensor_copy(den_sb[:], psum[:, 4, 0:CH]).then_inc(den_copied, 1)
                half4 = lambda ap: ap.rearrange("p (c n) -> p c n", n=CH)
                link(nc.vector.scalar_tensor_tensor(half4(work[0][:, 0:HN]), half4(none_row[:, cut]), h_sum,
                                                    psum[:, 0:4, 0:CH], ALU.mult, ALU.add))
                dve.wait_ge(den_spread, half + 1)
                link(nc.vector.scalar_tensor_tensor(half4(work[0][:, HN:2 * HN]), half4(none_row[:, cut]), float(N),
                                                    psum[:, 4:8, 0:CH], ALU.mult, ALU.add))
                link(nc.vector.reciprocal(work[0][:, HN:2 * HN], work[0][:, HN:2 * HN]))
                link(nc.vector.tensor_tensor(work[0][:, 0:HN], work[0][:, 0:HN], work[0][:, HN:2 * HN], ALU.mult))
                last = nc.vector.tensor_tensor(x_cur[:, cut], x_cur[:, cut], work[0][:, 0:HN], ALU.add)
                link(last)
                dve.nop().then_inc(half_done, 1)
            dve.nop().then_inc(x_ready, 1)
            layernorm(1)
            for n in range(2):
                dve.wait_ge(ln_out, n + 2)
                dve.wait_ge(nat_copied, n + 2)
                with dve.Fori(0, NT // 2) as g:
                    for j in range(2):
                        dve.wait_ge(sweep_added, n * NT + g * 2 + j + 1)
                        k = g * 2 + j
                        nc.vector.tensor_tensor(stat_k[j][:], x_nat[:, bass.ds(k * P, P)],
                                                x_nat[:, bass.ds(k * P, P)], ALU.max).then_inc(stat_ready, 1)
                if n == 0:
                    dve.wait_ge(sweep_done, 1)
                    nc.vector.tensor_tensor(chunks(work[0]), all8, chunks(recip_deg), ALU.mult).then_inc(sum_copied, 1)
                    nc.vector.tensor_tensor(bn_bias, vecs[:, 3:4], vecs[:, 4:5], ALU.add).then_inc(sum_copied, 1)
                    dve.wait_ge(dense_copied, 1)
                    link(nc.vector.tensor_reduce(bn_mean, work[1][:, 0:N], AX.X, ALU.add))
                    link(nc.vector.tensor_scalar(bn_mean, bn_mean, 1.0 / N, None, ALU.mult))
                    nc.vector.tensor_scalar(work[2], work[1], bn_mean, None, ALU.subtract).then_inc(bn_centered, 1)
                    dve.wait_ge(bn_squared, 2)
                    link(nc.vector.reciprocal(bn_std, bn_std))
                    nc.vector.tensor_tensor(bn_gain, bn_std, vecs[:, 5:6], ALU.mult).then_inc(bn_ready, 1)
                    dve.wait_ge(bn_out, 1)
                    nc.vector.tensor_tensor(x_cur, x_cur, work[0], ALU.add).then_inc(x_ready, 1)
                else:
                    dve.wait_ge(dense_made, 2)
                    nc.vector.scalar_tensor_tensor(chunks(x_cur), all8, vecs[:, 7:8], chunks(x_cur),
                                                   ALU.add, ALU.add).then_inc(x_ready, 1)
                layernorm(n + 2)


def kernel(**inputs):
    import numpy as np
    import concourse.bacc as bacc
    from concourse import mybir
    from concourse.bass_utils import run_bass_kernel_spmd

    n, padded, p = 3327, 3328, 128
    a = {k: np.asarray(v) for k, v in inputs.items()}
    lay = {}
    lay["xT"] = np.zeros((p, padded), a["x"].dtype)
    lay["xT"][:, :n] = a["x"].T
    lay["adjN"] = np.zeros((padded, padded), a["adj"].dtype)
    lay["adjN"][:n, :n] = a["adj"]
    lay["adjT"] = lay["adjN"].T
    for k in ("Wq", "Wk", "Wv"):
        lay[k] = a["L0_gnn_" + k].reshape(p, 8, p).transpose(2, 1, 0).reshape(p, 8 * p)
    lay["Wo"] = a["L0_gnn_Wo"].reshape(p, p, 8).transpose(1, 2, 0)
    w3 = a["L3_gnn_W"]
    mats = [a["L1_gnn_W"], a["L2_gnn_W_n"].T, a["L2_gnn_W_c"].T, w3[:, p:].T, w3[:, :p].T]
    lay["mats"] = np.stack(mats, axis=1)
    vecs = [a["L1_gnn_a1"], a["L1_gnn_a2"], np.broadcast_to(a["L1_gnn_a_bias"], (p,)), a["L2_gnn_b_n"],
            a["L2_gnn_b_c"], a["L2_gnn_gamma"], a["L2_gnn_beta"], a["L3_gnn_b"]]
    lay["vecs"] = np.stack(vecs, axis=1)
    nc = bacc.Bacc("TRN2", target_bir_lowering=False, num_devices=1)
    arrays, t = {}, {}
    for k, v in lay.items():
        arrays["in_" + k] = np.ascontiguousarray(v)
        t[k] = nc.dram_tensor("in_" + k, v.shape, mybir.dt.from_np(v.dtype), kind="ExternalInput").ap()
    out = nc.dram_tensor("out_T", (p, n), mybir.dt.float32, kind="ExternalOutput").ap()
    build(nc, t, out)
    got = run_bass_kernel_spmd(nc, [arrays], core_ids=[0])
    return np.ascontiguousarray(got.results[0]["out_T"].T)
```

```python
def build(nc, t, out):
    import numpy as np
    import concourse.bass as bass
    from concourse import mybir
    from contextlib import ExitStack

    fp32, bf16, i32 = mybir.dt.float32, mybir.dt.bfloat16, mybir.dt.int32
    ALU, ACT, AX = mybir.AluOpType, mybir.ActivationFunctionType, mybir.AxisListType

    P = 128
    N = 3327
    NT = 26
    NP = NT * P
    HEADS = 128
    F = 8
    TOK = NP * P
    SCALE = float(P) ** -0.5
    EPS = 1e-5

    NBLK = 4
    QB = NP // NBLK
    HALF = QB // 2
    QUART = QB // 4
    BT = NT // 2
    POOL_TILES = (1, 5, 10, 14, 18, 22)
    DVE_TILES = tuple(k for k in range(NT) if k not in POOL_TILES)
    RING = 13
    PAIR = 2 * NT
    PAIRS = HEADS // 2
    STORED = 4 * 16
    LAG_DVE, LAG_POOL = 5, 6
    HEADROOM = 40.0
    MASK = 2.0 ** 64
    SPAN = 120.0

    is_pool = lambda x: x % NT in POOL_TILES
    npool, ndve = 2 * len(POOL_TILES), 2 * len(DVE_TILES)
    pool_no = lambda x: (x // NT) * len(POOL_TILES) + POOL_TILES.index(x % NT)
    dve_no = lambda x: (x // NT) * len(DVE_TILES) + DVE_TILES.index(x % NT)
    av_key = lambda x: x + (LAG_POOL if is_pool(x) else LAG_DVE)
    av_order = sorted(range(PAIR), key=av_key)
    av_no = {x: n for n, x in enumerate(av_order)}

    ctx = ExitStack()
    with ctx:
        sb = lambda name, shape, dt=fp32: ctx.enter_context(nc.sbuf_tensor(name, shape, dt))
        sem = lambda name: ctx.enter_context(nc.semaphore(name))
        dram = lambda name, shape, dt: nc.dram_tensor(name, shape, dt, kind="Internal").ap()

        q_rows = dram("q_rows", (27, TOK), bf16)
        k_rows = dram("k_rows", (24, TOK), bf16)
        v_tok = dram("v_tok", (TOK, F + 1), fp32)
        o_rows = dram("o_rows", (F + 1, TOK), fp32)

        arena = sb("arena", [P, 12 * NP])
        big = lambda n: arena[:, n * NP:(n + 1) * NP]
        ident = sb("ident", [P, P])
        ones = sb("ones", [P, P])
        mean_w = sb("mean_w", [P, P])
        wo = sb("wo", [P, F, P])
        small = sb("small", [P, 64])
        recip_d = sb("recip_d", [P, 2, P])
        zeros = sb("zeros", [1, 512])
        flag = sb("flag", [1, 1], i32)

        slab = arena[:, 0:NT * QB].rearrange("p (k c) -> p k c", k=NT)
        ring = arena[:, NT * QB:(NT + RING) * QB].rearrange("p (k c) -> p k c", k=RING)
        kst = [sb(f"kst{j}", [P, NP], bf16) for j in range(2)]
        qst = [sb(f"qst{j}", [P, QB], bf16) for j in range(2)]
        vst = [sb(f"vst{j}", [P, NT * (F + 1)]) for j in range(2)]
        osb = [sb(f"osb{j}", [P, QUART]) for j in range(2)]

        at = [0]

        def piece(words):
            at[0] += words
            return arena[:, at[0] - words:at[0]]
        wqkv = [piece(F * P) for _ in range(3)]
        xblk = [piece(P) for _ in range(2)]
        parts = [[piece(3 * F * P // 2).bitcast(bf16).rearrange("p (a j) -> p a j", j=P) for _ in range(2)]
                 for _ in range(2)]
        resid = [piece(F * P) for _ in range(2)]
        square = [piece(F * P) for _ in range(2)]
        vtile = [piece(P * (F + 1)) for _ in range(2)]
        adj_s = [piece(NP) for _ in range(2)]
        q_norms, k_norms = piece(NP), piece(NP)
        rest = piece(NP)
        shift_parts = piece(3 * NP // 2).bitcast(bf16).rearrange("p (a c) -> p a c", a=3)
        assert at[0] <= 12 * NP
        stats = small[:, 0:3]
        gmax = small[:, 4:5]
        diag3 = small[:, 8:11]
        gstat = small[:, 12:15]
        roots = small[:, 16:18]
        neg_k, offset, crit, eps_t = (small[:, 20 + n:21 + n] for n in range(4))
        a_max = small[:, 32:32 + NT]

        g_adj, g_prob, g_prob_t = big(0), big(1), big(2)
        g_top, g_neg_max = small[:, 60:61], small[:, 61:62]

        oblk = [big(1)[:, 0:(F + 1) * P], big(2)[:, 0:(F + 1) * P]]
        yrow = [big(4)[:, j * F * P:(j + 1) * F * P] for j in range(2)]
        yblk = [big(3)[:, j * F * P:(j + 1) * F * P] for j in range(2)]
        x_cur = big(0)

        CH = NP // 8
        HN = NP // 2
        chunks = lambda ap: ap.rearrange("p (c n) -> p c n", n=CH)
        ln_d, ln_s = big(1), big(2)
        h_t, h_nat = big(1), big(2)
        a_row, b_row = big(3), big(4)
        x_nat = big(3)
        recip_deg, none_row = big(5), big(6)
        tile_buf = [big(7), big(8)]
        half_buf = [big(7 + i // 2)[:, i % 2 * HN:(i % 2 + 1) * HN] for i in range(4)]
        work = [big(9), big(10), big(11)]
        sweep_buf = [big(7), big(8), big(1), big(2)]
        s2_row = big(11)
        wmat = sb("wmat", [P, 5, P])
        vecs = sb("vecs", [P, 8])
        a1_all, a2_all = (sb(f"a{n}_all", [P, P]) for n in (1, 2))
        sel = sb("sel", [P, 4, P])
        stat_k = [sb(f"stat_k{j}", [P, P]) for j in range(2)]
        s2_pair = sb("s2_pair", [P, NT, 2])
        s2_now = [sb(f"s2_now{j}", [P, 2]) for j in range(2)]
        u_nat, deg_nat = sb("u_nat", [P, NT]), sb("deg_nat", [P, NT])
        u_now, zero_col = sb("u_now", [P, 2]), sb("zero_col", [P, 1])
        deg_now = [sb(f"deg_now{j}", [P, 1]) for j in range(2)]
        den_sb = sb("den_sb", [P, CH])
        ln_q = sb("ln_q", [P, 2 * CH])
        cols = sb("cols", [P, 16])
        s2_min, u_off, h_sum, bn_bias, bn_mean, bn_var, bn_std, bn_gain = (cols[:, n:n + 1] for n in range(8))
        psum = ctx.enter_context(nc.psum_tensor("psum", [P, 8, 512], fp32))
        ps_w = [psum[:, 2 * w:2 * w + 2, :] for w in range(3)]
        s_dve = [psum[:, 2 * b:2 * b + 2, 0:HALF] for b in range(2)]
        s_pool = psum[:, 4:6, 0:HALF]
        acc = [psum[:, 6 + j, 0:QUART] for j in range(2)]

        consts_in = sem("consts_in")
        setup = sem("setup")
        x_in = [sem(f"x_in{j}") for j in range(2)]
        adj_in = [sem(f"adj_in{j}") for j in range(2)]
        proj_done = [sem(f"proj_done{w}") for w in range(3)]
        part1 = [sem(f"part1_{w}") for w in range(2)]
        part2 = [sem(f"part2_{w}") for w in range(2)]
        part3 = [sem(f"part3_{w}") for w in range(2)]
        resid_done = [sem(f"resid_done{w}") for w in range(2)]
        square_free = [sem(f"square_free{w}") for w in range(2)]
        v_ready = sem("v_ready")
        adj_free = sem("adj_free")
        parts_out = [[sem(f"parts_out{w}{j}") for j in range(2)] for w in range(2)]
        v_out = [sem(f"v_out{j}") for j in range(2)]
        stats_ready = sem("stats_ready")
        stats_turned = sem("stats_turned")
        diag_ready = sem("diag_ready")
        stats_spread = sem("stats_spread")
        gstat_ready = sem("gstat_ready")
        roots_ready = sem("roots_ready")
        shift_ready = sem("shift_ready")
        dve_done = sem("dve_done")
        rows_out = sem("rows_out")
        psum_free = [*resid_done, v_ready]

        slab_in = [sem(f"slab_in{s}") for s in range(2)]
        head_in = [sem(f"head_in{j}") for j in range(2)]
        scores_dve = sem("scores_dve")
        scores_pool = sem("scores_pool")
        biased = sem("biased")
        exp_dve = sem("exp_dve")
        exp_pool = sem("exp_pool")
        bias_multiplied = sem("bias_multiplied")
        values_added = sem("values_added")
        acc_copied = sem("acc_copied")
        head_out = [sem(f"head_out{j}") for j in range(2)]

        flag_ready = sem("flag_ready")
        g_adj_in, g_in, g_scores, g_step, g_max, g_exp = (
            sem(n) for n in ("g_adj_in", "g_in", "g_scores", "g_step", "g_max", "g_exp"))
        g_turned, g_prob_copied, g_summed, g_out_ready, g_stored = (
            sem(n) for n in ("g_turned", "g_prob_copied", "g_summed", "g_out_ready", "g_stored"))
        recip_made = sem("recip_made")
        o_in = [sem(f"o_in{j}") for j in range(2)]
        y_ready = sem("y_ready")
        y_turned = sem("y_turned")
        yt_copied = sem("yt_copied")
        wo_done = sem("wo_done")
        x_row = sem("x_row")
        x_in2 = sem("x_in2")
        final_out = sem("final_out")
        ln_factor, ln_spread = sem("ln_factor"), sem("ln_spread")
        ln_mean, ln_centered, ln_squared, ln_var, ln_std, ln_out = (
            sem(n) for n in ("ln_mean", "ln_centered", "ln_squared", "ln_var", "ln_std", "ln_out"))
        x_ready = sem("x_ready")
        h_made, h_copied = sem("h_made"), sem("h_copied")
        s_made, s1_copied, s2_copied = sem("s_made"), sem("s1_copied"), sem("s2_copied")
        nat_made, nat_copied = sem("nat_made"), sem("nat_copied")
        tile_in = [sem(f"tile_in{j}") for j in range(2)]
        u_done, deg_done, deg_kept = sem("u_done"), sem("deg_done"), sem("deg_kept")
        neighbour_step = sem("neighbour_step")
        spread_in, spread_out = sem("spread_in"), sem("spread_out")
        half_in = [sem(f"half_in{j}") for j in range(4)]
        exponent_ready, weights_ready, gat_added = sem("exponent_ready"), sem("weights_ready"), sem("gat_added")
        gat_step = sem("gat_step")
        den_made, den_copied, den_spread, half_done = (
            sem(n) for n in ("den_made", "den_copied", "den_spread", "half_done"))
        stat_ready, sweep_added, sweep_done = sem("stat_ready"), sem("sweep_added"), sem("sweep_done")
        sweep_in = [sem(f"sweep_in{i}") for i in range(4)]
        sum_copied, dense_made, dense_copied = sem("sum_copied"), sem("dense_made"), sem("dense_copied")
        bn_centered, bn_squared, bn_ready, bn_out = (
            sem(n) for n in ("bn_centered", "bn_squared", "bn_ready", "bn_out"))

        block = ctx.enter_context(nc.Block())

        def rows_of(parts_dram, r0, nrows, rb):
            return parts_dram[r0:r0 + nrows, bass.ds(rb * (P * P), P * P)].rearrange("a (r j) -> r a j", j=P)

        def slot_free(eng, q, x):
            y = x - RING
            n = av_no[y] if y >= 0 else av_no[y + PAIR] - PAIR
            eng.wait_ge(values_added, (q + 1) * PAIR + n + 1)

        def for_tiles(eng, step):
            with eng.Fori(0, NT // 4) as g:
                for i in range(4):
                    step(g, i)
            for i in range(NT % 4):
                step(NT // 4, i)

        loads_of = lambda half, g, i: half * (NT // 4 + (i < NT % 4)) + g + 1

        @block.sync
        def _(sp):
            for w, name in enumerate(("Wq", "Wk", "Wv")):
                sp.dma_start(wqkv[w], t[name]).then_inc(consts_in, 16)
            sp.dma_start(wo[:], t["Wo"]).then_inc(consts_in, 16)
            sp.dma_start(wmat[:], t["mats"]).then_inc(consts_in, 16)
            sp.dma_start(vecs[:], t["vecs"]).then_inc(consts_in, 16)
            sp.wait_ge(setup, 12)
            sp.dma_start(o_rows[:, TOK - P:TOK], ones[0:F + 1, :]).then_inc(rows_out, 16)
            with sp.Fori(0, NT // 2) as g:
                for j in range(2):
                    sp.wait_ge(proj_done[2], g * 2 + j + 1)
                    sp.dma_start(xblk[j], t["xT"][:, bass.ds((g * 2 + j) * P, P)]).then_inc(x_in[j], 16)
                    sp.wait_ge(adj_free, g * 2 + j + 1)
                    sp.dma_start(adj_s[j], t["adjN"][bass.ds((g * 2 + j) * P, P), :]).then_inc(adj_in[j], 16)
                    if j == 1:
                        for jj in range(2):
                            rb = g * 2 + jj
                            for w in range(2):
                                sp.wait_ge(part3[w], rb + 2)
                                sp.dma_start(rows_of((q_rows, k_rows)[w], 0, 24, rb), parts[w][jj][:])\
                                    .then_inc(parts_out[w][jj], 16)
                            sp.wait_ge(v_ready, rb + 2)
                            sp.dma_start(v_tok[bass.ds(rb * (P * P), P * P), :]
                                         .rearrange("(r j) f -> r (j f)", j=P), vtile[jj]).then_inc(v_out[jj], 16)
            sp.wait_ge(shift_ready, 1)
            for a in range(3):
                sp.dma_start(q_rows[24 + a, :].rearrange("(b r j) -> r b j", r=P, j=P),
                             shift_parts[:, a, :].rearrange("p (b j) -> p b j", j=P)).then_inc(rows_out, 16)
            sp.wait_ge(rows_out, 64)
            for w in range(2):
                for j in range(2):
                    sp.wait_ge(parts_out[w][j], 16 * (NT // 2 + 1))
            for j in range(2):
                sp.wait_ge(v_out[j], 16 * (NT // 2 + 1))

            def load_keys(key0, j, loaded):
                for r in range(3):
                    sp.dma_start(kst[j][8 * r:8 * r + 8, :], k_rows[0:8, bass.ds(key0, NP)]).then_inc(loaded, 16)
                for r in range(2):
                    sp.dma_start(kst[j][27 + 8 * r:35 + 8 * r, :], k_rows[8:16, bass.ds(key0, NP)])\
                        .then_inc(loaded, 16)
                sp.dma_start(kst[j][43:51, :], k_rows[16:24, bass.ds(key0, NP)]).then_inc(loaded, 16)

            def load_values(key0, j, loaded):
                W = BT * (F + 1)
                v = v_tok[bass.ds(key0, NP), :].rearrange("(s p b) f -> s p (b f)", s=2, p=P)
                sp.dma_start(vst[j][:, 0:W], v[0]).then_inc(loaded, 16)
                sp.dma_start(vst[j][0:P - 1, W:2 * W], v[1, 0:P - 1]).then_inc(loaded, 16)
                sp.dma_start(vst[j][P - 1:P, W:2 * W - (F + 1)], v[1, P - 1:P, 0:W - (F + 1)]).then_inc(loaded, 16)

            def load_head(col0, h, j):
                q0 = h * N + col0
                load_keys(h * N, j, head_in[j])
                sp.dma_start(qst[j][0:27, :], q_rows[0:27, bass.ds(q0, QB)]).then_inc(head_in[j], 16)
                sp.dma_start(qst[j][27:43, :], q_rows[0:16, bass.ds(q0, QB)]).then_inc(head_in[j], 16)
                sp.dma_start(qst[j][43:51, :], q_rows[0:8, bass.ds(q0, QB)]).then_inc(head_in[j], 16)
                load_values(h * N, j, head_in[j])

            def store_head(col0, h, j):
                o0 = h * N + col0
                for c in range(4):
                    sp.dma_start(o_rows[:, bass.ds(o0 + c * QUART, QUART)], osb[j][32 * c:32 * c + F + 1, :])\
                        .then_inc(head_out[j], 16)

            sp.wait_ge(flag_ready, 1)
            narrow = sp.value_load(flag[0:1, 0:1], min_val=0, max_val=1)
            with sp.If(narrow == 1):
                def load_slab(col0, s):
                    sp.dma_start(slab[:, s * BT:(s + 1) * BT, :],
                                 t["adjT"][s * BT * P:(s + 1) * BT * P, bass.ds(col0, QB)]
                                 .rearrange("(p b) c -> p b c", p=P)).then_inc(slab_in[s], 16)

                def pass_of_heads(nb, last):
                    col0 = nb * (-QB) + (NBLK - 1) * QB
                    q0 = nb * PAIRS
                    with sp.Fori(0, PAIRS - 1) as p:
                        for j in range(2):
                            sp.wait_ge(values_added, (q0 + p + 1) * PAIR + (j + 1) * NT)
                            load_head(col0, (p + 1) * 2 + j, j)
                            sp.wait_ge(acc_copied, (q0 + p) * 2 + j + 2)
                            store_head(col0, p * 2 + j, j)
                    q1 = q0 + PAIRS - 1
                    for j in range(2):
                        sp.wait_ge(values_added, (q1 + 1) * PAIR + (j + 1) * NT)
                        if j == 1 and not last:
                            load_slab(nb * (-QB) + (NBLK - 2) * QB, 1)
                        if not last:
                            load_head(nb * (-QB) + (NBLK - 2) * QB, j, j)
                        if j == 0 and not last:
                            sp.wait_ge(values_added, (q1 + 1) * PAIR + max(av_no[NT + k] for k in range(BT)) + 1)
                        sp.wait_ge(acc_copied, q1 * 2 + j + 2)
                        store_head(col0, HEADS - 2 + j, j)
                        if j == 0 and not last:
                            load_slab(nb * (-QB) + (NBLK - 2) * QB, 0)

                for j in range(2):
                    sp.nop().then_inc(head_out[j], STORED + 16)
                for s in range(2):
                    load_slab((NBLK - 1) * QB, s)
                for j in range(2):
                    load_head((NBLK - 1) * QB, j, j)
                with sp.Fori(0, NBLK - 1) as nb:
                    pass_of_heads(nb, False)
                pass_of_heads(NBLK - 1, True)
                for j in range(2):
                    sp.wait_ge(head_out[j], (NBLK * PAIRS + 1) * STORED + 16)
            with sp.Else():
                sp.nop().then_inc(g_stored, 16)
                with sp.Fori(0, NT) as i:
                    row0 = i * (-P) + (NT - 1) * P
                    sp.dma_start(g_adj, t["adjN"][bass.ds(row0, P), :]).then_inc(g_adj_in, 16)
                    with sp.Fori(0, HEADS) as h:
                        step = i * HEADS + h
                        sp.wait_ge(g_summed, step + 1)
                        load_keys(h * N, 0, g_in)
                        load_values(h * N, 0, g_in)
                        for r0, rows in ((0, 24), (27, 16), (43, 8)):
                            sp.dma_start(qst[0][r0:r0 + rows, 0:P], q_rows[0:rows, bass.ds(h * N + row0, P)])\
                                .then_inc(g_in, 16)
                        sp.wait_ge(g_out_ready, step + 2)
                        sp.dma_start(o_rows[:, bass.ds((NT - 1) * P + h * N - i * P, P)], osb[0][0:F + 1, 0:P])\
                            .then_inc(g_stored, 16)
                sp.wait_ge(g_stored, NT * HEADS * 16 + 16)

            sp.dma_start(x_cur, t["xT"]).then_inc(x_in2, 16)
            with sp.Fori(0, NT // 2) as g:
                for j in range(2):
                    sp.wait_ge(y_ready, g * 2 + j + 1)
                    sp.dma_start(oblk[j].rearrange("p (f j) -> p f j", j=P), rows_of(o_rows, 0, F + 1, g * 2 + j))\
                        .then_inc(o_in[j], 16)
            sp.wait_ge(ln_out, 1)
            with sp.Fori(0, NT // 2) as g:
                for j in range(2):
                    sp.wait_ge(u_done, g * 2 + j + 1)
                    sp.wait_ge(deg_done, g * 2 + j + 1)
                    sp.dma_start(tile_buf[j], t["adjN"][bass.ds((g * 2 + j) * P, P), :]).then_inc(tile_in[j], 16)
            sp.wait_ge(u_done, NT + 2)
            sp.wait_ge(deg_done, NT + 2)

            for half in range(2):
                if half == 1:
                    sp.wait_ge(exponent_ready, NT + 4)

                def load_half(g, i):
                    sp.wait_ge(exponent_ready, half * NT + g * 4 + i + 1)
                    sp.dma_start(half_buf[i], t["adjT"][bass.ds((g * 4 + i) * P, P), half * HN:(half + 1) * HN])\
                        .then_inc(half_in[i], 16)

                for_tiles(sp, load_half)
            sp.wait_ge(exponent_ready, 2 * NT + 4)
            for n, name in enumerate(("adjN", "adjT")):
                if n == 1:
                    sp.wait_ge(sweep_added, NT + 4)

                def load_rows(g, i):
                    if i == 2:
                        sp.wait_ge(ln_out, n + 2)
                    sp.wait_ge(sweep_added, n * NT + g * 4 + i + 1)
                    sp.dma_start(sweep_buf[i], t[name][bass.ds((g * 4 + i) * P, P), :]).then_inc(sweep_in[i], 16)

                for_tiles(sp, load_rows)
            sp.wait_ge(ln_out, 4)
            sp.dma_start(out, x_cur[:, 0:N]).then_inc(final_out, 16)
            sp.wait_ge(final_out, 16)

        @block.gpsimd
        def _(pool):
            pool.wait_ge(setup, 11)
            nc.gpsimd.affine_select(out=ident[:], in_=ident[:], compare_op=ALU.not_equal, fill=1.0, base=0,
                                    pattern=[[-1, P]], channel_multiplier=1).then_inc(setup, 1)
            pool.wait_ge(flag_ready, 1)
            narrow = pool.value_load(flag[0:1, 0:1], min_val=0, max_val=1)
            with pool.If(narrow == 1):
                with pool.Fori(0, NBLK) as nb:
                    with pool.Fori(0, PAIRS) as p:
                        for x in range(PAIR):
                            if is_pool(x):
                                pool.wait_ge(exp_pool, (nb * PAIRS + p) * npool + pool_no(x) + 2)
                                nc.gpsimd.tensor_tensor(ring[:, x % RING, :], ring[:, x % RING, :], slab[:, x % NT, :],
                                                        ALU.mult).then_inc(bias_multiplied, 1)

        @block.tensor
        def _(pe):
            pe.wait_ge(setup, 12)
            pe.wait_ge(consts_in, 96)
            pe.nop().then_inc(proj_done[2], 2)
            with pe.Fori(0, NT // 2) as g:
                for j in range(2):
                    pe.wait_ge(x_in[j], (g + 1) * 16)
                    for w in range(3):
                        pe.wait_ge(psum_free[w], g * 2 + j + 1)
                        for c in range(2):
                            last = nc.tensor.matmul(ps_w[w][:, c, :], xblk[j], wqkv[w][:, c * 512:(c + 1) * 512],
                                                    start=True, stop=True)
                        last.then_inc(proj_done[w], 1)
            pe.wait_ge(stats_ready, 1)
            nc.tensor.transpose(psum[0:3, 0, 0:P], stats, ident[:]).then_inc(stats_turned, 1)
            pe.wait_ge(diag_ready, 1)
            nc.tensor.matmul(psum[:, 1, 0:3], ones[0:3, :], diag3[0:3, :], start=True, stop=True)\
                .then_inc(stats_spread, 1)

            def scores(x, q):
                j, k = divmod(x, NT)
                if k == 0:
                    pe.wait_ge(head_in[j], (q + 1) * (12 * 16))
                s, b = divmod(k, BT)
                keys = kst[j][:, s * BT * P:(s + 1) * BT * P].rearrange("r (p b) -> r b p", b=BT)[:, b, :]
                if is_pool(x):
                    dst, n = s_pool, pool_no(x)
                    pe.wait_ge(exp_pool, q * npool + n + 1)
                else:
                    n = dve_no(x)
                    dst = s_dve[n % 2]
                    pe.wait_ge(biased, q * ndve + n + 1)
                for c in range(2):
                    last = nc.tensor.matmul(dst[:, c, :], keys, qst[j][:, c * HALF:(c + 1) * HALF],
                                            start=True, stop=True)
                last.then_inc(scores_pool if is_pool(x) else scores_dve, 1)

            def values(x, q):
                j, k = divmod(x, NT)
                if is_pool(x):
                    pe.wait_ge(bias_multiplied, q * npool + pool_no(x) + 1)
                else:
                    pe.wait_ge(exp_dve, q * ndve + dve_no(x) + 1)
                for c in range(4):
                    last = nc.tensor.matmul(acc[j][32 * c:32 * c + F + 1, :], vst[j][:, k * (F + 1):(k + 1) * (F + 1)],
                                            ring[:, x % RING, c * QUART:(c + 1) * QUART],
                                            start=(k == 0), stop=(av_order[NT - 1 + j * NT] == x))
                last.then_inc(values_added, 1)

            assert all(x // NT == n // NT for n, x in enumerate(av_order))

            def pair(q, first):
                for x in range(PAIR):
                    scores(x, q)
                    for y in av_order:
                        if not first and x - 1 < av_key(y) - PAIR <= x:
                            values(y, q - 1)
                    for y in av_order:
                        if x - 1 < av_key(y) <= x:
                            values(y, q)

            pe.wait_ge(flag_ready, 1)
            narrow = pe.value_load(flag[0:1, 0:1], min_val=0, max_val=1)
            with pe.If(narrow == 1):
                for j in range(2):
                    last = nc.tensor.matmul(acc[j], ones[0:1, :], zeros[:, 0:QUART], start=True, stop=True)
                last.then_inc(values_added, PAIR)
                pair(0, True)
                with pe.Fori(1, NBLK * PAIRS) as q:
                    pair(q, False)
                for y in av_order:
                    if av_key(y) > PAIR - 1:
                        values(y, NBLK * PAIRS - 1)
            with pe.Else():
                pe.nop().then_inc(g_summed, 1)
                with pe.Fori(0, NT) as i:
                    with pe.Fori(0, HEADS) as h:
                        step = i * HEADS + h
                        pe.wait_ge(g_in, (step + 1) * (12 * 16))
                        pe.wait_ge(g_out_ready, step + 1)
                        for c in range(8):
                            last = nc.tensor.matmul(psum[:, c, 0:CH], qst[0][:, 0:P], kst[0][:, c * CH:(c + 1) * CH],
                                                    start=True, stop=True)
                        last.then_inc(g_scores, 1)
                        pe.wait_ge(g_exp, step + 1)
                        for k in range(NT):
                            hs, b = divmod(k, BT)
                            keys = g_prob[:, hs * BT * P:(hs + 1) * BT * P].rearrange("n (p b) -> n b p", b=BT)
                            last = nc.tensor.transpose(psum[:, k // 4, (k % 4) * P:(k % 4 + 1) * P], keys[:, b, :],
                                                       ident[:])
                        last.then_inc(g_turned, 1)
                        pe.wait_ge(g_prob_copied, step + 1)
                        for k in range(NT):
                            last = nc.tensor.matmul(psum[0:F + 1, 7, 0:P], vst[0][:, k * (F + 1):(k + 1) * (F + 1)],
                                                    g_prob_t[:, k * P:(k + 1) * P], start=(k == 0), stop=(k == NT - 1))
                        last.then_inc(g_summed, 1)

            pe.nop().then_inc(sweep_added, 4)
            pe.nop().then_inc(y_turned, 2)
            pe.nop().then_inc(wo_done, 2)

            def turn(g, j):
                pe.wait_ge(y_ready, g * 2 + j + 3)
                pe.wait_ge(yt_copied, g * 2 + j + 1)
                for f in range(F):
                    last = nc.tensor.transpose(psum[:, 4 * j + f // 4, (f % 4) * P:(f % 4 + 1) * P],
                                               yrow[j][:, f * P:(f + 1) * P], ident[:])
                last.then_inc(y_turned, 1)

            def project(g, j):
                pe.wait_ge(yt_copied, g * 2 + j + 3)
                pe.wait_ge(x_row, g * 2 + j + 1)
                for f in range(F):
                    last = nc.tensor.matmul(psum[:, 2 + j, 0:P], wo[:, f, :], yblk[j][:, f * P:(f + 1) * P],
                                            start=(f == 0), stop=(f == F - 1))
                last.then_inc(wo_done, 1)

            turn(0, 0)
            with pe.Fori(0, NT // 2 - 1) as g:
                turn(g, 1)
                project(g, 0)
                turn(g + 1, 0)
                project(g, 1)
            turn(NT // 2 - 1, 1)
            project(NT // 2 - 1, 0)
            project(NT // 2 - 1, 1)

            def turned_sums(lhs, rhs, first=True, last=True):
                for c in range(8):
                    out_ = nc.tensor.matmul(psum[:, c, 0:CH], lhs, rhs[:, c * CH:(c + 1) * CH], start=first,
                                            stop=last, skip_group_check=True)
                return out_

            def layernorm(n):
                pe.wait_ge(x_ready, n + 1)
                turned_sums(mean_w[:], x_cur).then_inc(ln_mean, 1)
                pe.wait_ge(ln_squared, n + 1)
                for b in range(2):
                    for c in range(4):
                        last = nc.tensor.matmul(psum[32 * c:32 * c + 32, b, 0:CH], mean_w[:, 0:32],
                                                ln_s[:, (2 * c + b) * CH:(2 * c + b + 1) * CH], start=True, stop=True)
                last.then_inc(ln_var, 1)
                pe.wait_ge(ln_factor, n + 1)
                for c in range(4):
                    for b in range(2):
                        last = nc.tensor.matmul(psum[:, 2 * c + b, 0:CH], sel[:, c, :], ln_q[:, b * CH:(b + 1) * CH],
                                                start=True, stop=True)
                last.then_inc(ln_spread, 1)

            def by_node(src):
                for k in range(NT):
                    last = nc.tensor.transpose(psum[:, k // 4, (k % 4) * P:(k % 4 + 1) * P],
                                               src[:, k * P:(k + 1) * P], ident[:])
                last.then_inc(nat_made, 1)

            def zero_banks(n, stop=False):
                for c in range(n):
                    last = nc.tensor.matmul(psum[:, c, 0:CH], ones[0:1, :], zeros[:, 0:CH], start=not stop, stop=stop,
                                            skip_group_check=True)
                return last

            layernorm(0)
            pe.wait_ge(ln_out, 1)
            turned_sums(wmat[:, 0, :], x_cur).then_inc(h_made, 1)
            pe.wait_ge(h_copied, 1)
            turned_sums(a1_all[:], h_t).then_inc(s_made, 1)
            pe.wait_ge(s1_copied, 1)
            turned_sums(a2_all[:], h_t).then_inc(s_made, 1)
            pe.wait_ge(s2_copied, 1)
            for k in range(NT):
                nc.tensor.matmul(psum[:, k // 4, (k % 4) * P:(k % 4 + 1) * P], x_cur[:, k * P:(k + 1) * P],
                                 wmat[:, 0, :], start=True, stop=True)
            for k in range(NT):
                last = nc.tensor.matmul(psum[:, 7, k:k + 1], h_t[:, k * P:(k + 1) * P], vecs[:, 1:2],
                                        start=True, stop=True)
            last.then_inc(nat_made, 1)
            for n in range(2):
                pe.wait_ge(spread_in, n + 1)
                turned_sums(ones[:], work[0]).then_inc(spread_out, 1)
            for half in range(2):
                if half == 0:
                    pe.wait_ge(spread_in, 3)
                else:
                    pe.wait_ge(half_done, half)
                zero_banks(5)
                if half == 0:
                    pe.nop().then_inc(gat_added, 2)
                with pe.Fori(0, NT // 2) as g:
                    for j in range(2):
                        r = half * NT + g * 2 + j
                        pe.wait_ge(weights_ready, r + 1)
                        for c in range(4):
                            nc.tensor.matmul(psum[:, c, 0:CH], stat_k[j][:], work[j][:, c * CH:(c + 1) * CH],
                                             start=False, stop=False, skip_group_check=True)
                        for c in range(4):
                            last = nc.tensor.matmul(psum[32 * c:32 * c + 9, 4, 0:CH], ones[:, 0:9],
                                                    work[j][:, c * CH:(c + 1) * CH], start=False, stop=False,
                                                    skip_group_check=True)
                        last.then_inc(gat_added, 1)
                zero_banks(5, stop=True).then_inc(den_made, 1)
                pe.wait_ge(den_copied, half + 1)
                for c in range(4):
                    last = nc.tensor.matmul(psum[:, 4 + c, 0:CH], sel[:, c, :], den_sb[:], start=True, stop=True)
                last.then_inc(den_spread, 1)
            layernorm(1)
            for n in range(2):
                pe.wait_ge(ln_out, n + 2)
                by_node(x_cur)
                pe.wait_ge(nat_copied, n + 2)
                zero_banks(8)

                def add_tile(g, i):
                    pe.wait_ge(sweep_in[i], loads_of(n, g, i) * 16)
                    pe.wait_ge(stat_ready, n * NT + g * 4 + i + 1)
                    for c in range(8):
                        last = nc.tensor.matmul(psum[:, c, 0:CH], stat_k[i % 2][:],
                                                sweep_buf[i][:, c * CH:(c + 1) * CH],
                                                start=False, stop=False, skip_group_check=True)
                    last.then_inc(sweep_added, 1)

                for_tiles(pe, add_tile)
                zero_banks(8, stop=True).then_inc(sweep_done, 1)
                pe.wait_ge(sum_copied, 2 * n + 1)
                for c in range(8):
                    nc.tensor.matmul(psum[:, c, 0:CH], wmat[:, 1 + 2 * n, :], work[0][:, c * CH:(c + 1) * CH],
                                     start=True, stop=False)
                    last = nc.tensor.matmul(psum[:, c, 0:CH], wmat[:, 2 + 2 * n, :], x_cur[:, c * CH:(c + 1) * CH],
                                            start=False, stop=True)
                last.then_inc(dense_made, 1)
                layernorm(n + 2)

        @block.scalar
        def _(act):
            act.wait_ge(setup, 12)
            act.nop().then_inc(v_ready, 1)
            for j in range(2):
                act.nop().then_inc(parts_out[0][j], 16)
                act.nop().then_inc(parts_out[1][j], 16)
                act.nop().then_inc(v_out[j], 16)
            with act.Fori(0, NT // 2) as g:
                for j in range(2):
                    for w in range(2):
                        act.wait_ge(proj_done[w], g * 2 + j + 1)
                        act.wait_ge(square_free[w], g * 2 + j + 1)
                        nc.scalar.activation(square[w].rearrange("p (b c) -> p b c", b=2), ps_w[w], ACT.Square)
                        act.wait_ge(parts_out[w][j], (g + 1) * 16)
                        nc.scalar.copy(parts[w][j][:, 0:8, :].rearrange("p (b f) c -> p b (f c)", b=2), ps_w[w])\
                            .then_inc(part1[w], 1)
                    for w in range(2):
                        act.wait_ge(resid_done[w], g * 2 + j + 2)
                        nc.scalar.copy(parts[w][j][:, 8:16, :].rearrange("p f c -> p (f c)"), resid[w]).then_inc(part2[w], 1)
                    act.wait_ge(proj_done[2], g * 2 + j + 3)
                    act.wait_ge(v_out[j], (g + 1) * 16)
                    for b in range(2):
                        last = nc.scalar.copy(vtile[j].rearrange("p (t f) -> p f t", f=F + 1)[:, 4 * b:4 * b + 4, :],
                                              ps_w[2][:, b, :].rearrange("p (f t) -> p f t", t=P))
                    last.then_inc(v_ready, 1)
            act.wait_ge(gstat_ready, 1)
            nc.scalar.activation(roots, gstat[:, 0:2], ACT.Sqrt).then_inc(roots_ready, 1)
            nc.scalar.activation(q_norms, q_norms, ACT.Sqrt).then_inc(roots_ready, 1)

            def exp_slab(nb, s):
                act.wait_ge(slab_in[s], (nb + 1) * 16)
                for k in POOL_TILES:
                    if k // BT == s:
                        nc.scalar.activation(slab[:, k, :], slab[:, k, :], ACT.Exp, scale=2.0)

            def act_pair(nb, q, first):
                for x in act_order:
                    if first and x in (POOL_TILES[0], min(k for k in POOL_TILES if k >= BT)):
                        exp_slab(nb, x // BT)
                    if is_pool(x):
                        act.wait_ge(scores_pool, q * npool + pool_no(x) + 1)
                        slot_free(act, q, x)
                        nc.scalar.activation(ring[:, x % RING, :].rearrange("p (u c) -> p u c", u=2), s_pool,
                                             ACT.Exp, scale=SCALE).then_inc(exp_pool, 1)
                    else:
                        act.wait_ge(biased, q * ndve + dve_no(x) + 3)
                        nc.scalar.activation(ring[:, x % RING, :], ring[:, x % RING, :], ACT.Exp,
                                             scale=2.0).then_inc(exp_dve, 1)

            act_order = sorted(range(PAIR), key=lambda x: x + (0.1 if is_pool(x) else 2))
            act.wait_ge(flag_ready, 1)
            narrow = act.value_load(flag[0:1, 0:1], min_val=0, max_val=1)
            with act.If(narrow == 1):
                act.nop().then_inc(exp_pool, 1)
                with act.Fori(0, NBLK) as nb:
                    act_pair(nb, nb * PAIRS, True)
                    with act.Fori(1, PAIRS) as p:
                        act_pair(nb, nb * PAIRS + p, False)
            with act.Else():
                with act.Fori(0, NT) as i:
                    with act.Fori(0, HEADS) as h:
                        step = i * HEADS + h
                        act.wait_ge(g_max, step + 1)
                        nc.scalar.activation(g_prob[:, 0:N], g_prob[:, 0:N], ACT.Exp, bias=g_neg_max).then_inc(g_exp, 1)
                        act.wait_ge(g_turned, step + 1)
                        nc.scalar.copy(g_prob_t[:, 0:24 * P].rearrange("p (b c) -> p b c", c=512), psum[:, 0:6, :])
                        nc.scalar.copy(g_prob_t[:, 24 * P:NP], psum[:, 6, 0:2 * P]).then_inc(g_prob_copied, 1)

            act.nop().then_inc(yt_copied, 2)
            with act.Fori(0, NT // 2) as g:
                for j in range(2):
                    act.wait_ge(y_turned, g * 2 + j + 3)
                    act.wait_ge(wo_done, g * 2 + j + 1)
                    nc.scalar.copy(yblk[j].rearrange("p (b c) -> p b c", b=2), psum[:, 4 * j:4 * j + 2, :])\
                        .then_inc(yt_copied, 1)

            all8 = psum[:, :, 0:CH]

            def layernorm(n):
                act.wait_ge(ln_centered, n + 1)
                nc.scalar.activation(ln_s, ln_d, ACT.Square).then_inc(ln_squared, 1)
                act.wait_ge(ln_var, n + 1)
                nc.scalar.activation(chunks(ln_q[:]), psum[:, 0:2, 0:CH], ACT.Sqrt, bias=eps_t).then_inc(ln_std, 1)

            def copy_by_node(dst):
                nc.scalar.copy(dst[:, 0:24 * P].rearrange("p (b c) -> p b c", c=512), psum[:, 0:6, :])
                return nc.scalar.copy(dst[:, 24 * P:NP], psum[:, 6, 0:2 * P])

            layernorm(0)
            act.wait_ge(h_made, 1)
            nc.scalar.copy(chunks(h_t), all8).then_inc(h_copied, 1)
            act.wait_ge(s_made, 2)
            nc.scalar.copy(chunks(s2_row), all8).then_inc(s2_copied, 1)
            act.wait_ge(nat_made, 1)
            copy_by_node(h_nat)
            nc.scalar.copy(s2_pair[:, :, 0], psum[:, 7, 0:NT]).then_inc(nat_copied, 1)
            act.nop().then_inc(deg_done, 2)
            with act.Fori(0, NT // 2) as g:
                for j in range(2):
                    act.wait_ge(tile_in[j], (g + 1) * 16)
                    act.wait_ge(deg_kept, g * 2 + j + 1)
                    act.wait_ge(deg_done, g * 2 + j + 2)
                    nc.scalar.activation(work[1], tile_buf[j], ACT.Copy, accum_out=deg_now[j][:])\
                        .then_inc(deg_done, 1)
            for half in range(2):
                with act.Fori(0, NT // 2) as g:
                    for j in range(2):
                        act.wait_ge(exponent_ready, half * NT + g * 2 + j + 5)
                        nc.scalar.activation(work[j][:, 0:HN], work[j][:, 0:HN], ACT.Exp, scale=-MASK)\
                            .then_inc(weights_ready, 1)
            layernorm(1)
            act.wait_ge(nat_made, 2)
            copy_by_node(x_nat).then_inc(nat_copied, 1)
            act.wait_ge(dense_made, 1)
            act.wait_ge(sum_copied, 2)
            nc.scalar.activation(chunks(work[1]), all8, ACT.Identity, bias=bn_bias).then_inc(dense_copied, 1)
            act.wait_ge(bn_centered, 1)
            nc.scalar.activation(work[0][:, 0:N], work[2][:, 0:N], ACT.Square, accum_out=bn_var).then_inc(bn_squared, 1)
            act.wait_ge(bn_squared, 1)
            nc.scalar.activation(bn_std, bn_var, ACT.Sqrt, scale=1.0 / N, bias=eps_t).then_inc(bn_squared, 1)
            act.wait_ge(bn_ready, 1)
            nc.scalar.activation(work[0], work[2], ACT.Relu, scale=bn_gain, bias=vecs[:, 6:7]).then_inc(bn_out, 1)
            layernorm(2)
            act.wait_ge(nat_made, 3)
            copy_by_node(x_nat).then_inc(nat_copied, 1)
            act.wait_ge(sweep_done, 2)
            nc.scalar.copy(chunks(work[0]), all8).then_inc(sum_copied, 1)
            layernorm(3)

        @block.vector
        def _(dve):
            done = [0]

            def link(ins):
                done[0] += 1
                ins.then_inc(dve_done, 1)
                dve.wait_ge(dve_done, done[0])

            nc.vector.memset(ones[:], 1.0).then_inc(setup, 1)
            for j in range(2):
                nc.vector.memset(vst[j][:], 0.0).then_inc(setup, 1)
                nc.vector.memset(kst[j][:], 1.0).then_inc(setup, 1)
                nc.vector.memset(qst[j][:], 0.0).then_inc(setup, 1)
                nc.vector.memset(vtile[j], 1.0).then_inc(setup, 1)
            nc.vector.memset(mean_w[:], 1.0 / P)
            nc.vector.memset(zeros[:], 0.0)
            nc.vector.memset(zero_col[:], 0.0)
            nc.vector.memset(eps_t, EPS).then_inc(setup, 1)
            nc.vector.memset(ident[:], 0.0).then_inc(setup, 1)
            for s in (*resid_done, *square_free, *part3):
                dve.nop().then_inc(s, 1)
            dve.nop().then_inc(adj_free, 2)

            dve.wait_ge(consts_in, 96)
            dve.wait_ge(setup, 12)
            nc.vector.tensor_scalar(a1_all[:], ones[:], vecs[:, 0:1], None, ALU.mult)
            nc.vector.tensor_scalar(a2_all[:], ones[:], vecs[:, 1:2], None, ALU.mult)
            for c in range(4):
                nc.vector.tensor_scalar(sel[:, c, :], ones[:], ident[:, 32 * c:32 * c + 1], None, ALU.mult)

            with dve.Fori(0, NT // 2) as g:
                for j in range(2):
                    r = g * 2 + j
                    for w in range(2):
                        dve.wait_ge(part3[w], r + 1)
                        dve.wait_ge(part1[w], r + 1)
                        nc.vector.tensor_tensor(resid[w].rearrange("p (b c) -> p b c", b=2), ps_w[w],
                                                parts[w][j][:, 0:8, :].rearrange("p (b f) c -> p b (f c)", b=2),
                                                ALU.subtract).then_inc(resid_done[w], 1)
                    for w, norms in enumerate((q_norms, k_norms)):
                        nc.vector.tensor_reduce(norms[:, bass.ds(r * P, P)],
                                                square[w].rearrange("p (f t) -> p t f", t=P),
                                                AX.X, ALU.add).then_inc(square_free[w], 1)
                    dve.wait_ge(adj_in[j], (g + 1) * 16)
                    for w in range(2):
                        dve.wait_ge(part2[w], r + 1)
                        nc.vector.tensor_tensor(parts[w][j][:, 16:24, :].rearrange("p f c -> p (f c)"), resid[w],
                                                parts[w][j][:, 8:16, :].rearrange("p f c -> p (f c)"),
                                                ALU.subtract).then_inc(part3[w], 1)
                    nc.vector.tensor_reduce(a_max[:, bass.ds(r, 1)], adj_s[j], AX.X, ALU.max,
                                            apply_absolute_value=True).then_inc(adj_free, 1)

            dve.wait_ge(adj_free, NT + 2)
            dve.wait_ge(square_free[1], NT + 1)
            dve.wait_ge(square_free[0], NT + 1)
            nc.vector.tensor_reduce(stats[:, 0:1], k_norms, AX.X, ALU.max)
            nc.vector.tensor_reduce(stats[:, 1:2], q_norms, AX.X, ALU.max)
            nc.vector.tensor_reduce(stats[:, 2:3], a_max, AX.X, ALU.max).then_inc(stats_ready, 1)
            dve.wait_ge(stats_turned, 1)
            link(nc.vector.tensor_reduce(gmax[0:3, :], psum[0:3, 0, 0:P], AX.X, ALU.max))
            nc.vector.tensor_scalar(diag3[0:3, :], ident[0:3, 0:3], gmax[0:3, :], None, ALU.mult)\
                .then_inc(diag_ready, 1)
            dve.wait_ge(stats_spread, 1)
            nc.vector.tensor_copy(gstat, psum[:, 1, 0:3]).then_inc(gstat_ready, 1)
            dve.wait_ge(gstat_ready, 1)
            link(nc.vector.tensor_scalar(offset, gstat[:, 2:3], -2.0 / SCALE, HEADROOM / SCALE, ALU.mult, ALU.add))
            dve.wait_ge(roots_ready, 2)
            link(nc.vector.tensor_scalar(neg_k, roots[:, 0:1], -1.0, None, ALU.mult))
            link(nc.vector.tensor_scalar(q_norms, q_norms, neg_k, offset, ALU.mult, ALU.add))
            link(nc.vector.tensor_copy(shift_parts[:, 0, :], q_norms))
            link(nc.vector.tensor_tensor(rest, q_norms, shift_parts[:, 0, :], ALU.subtract))
            link(nc.vector.tensor_copy(shift_parts[:, 1, :], rest))
            nc.vector.tensor_tensor(shift_parts[:, 2, :], rest, shift_parts[:, 1, :], ALU.subtract)\
                .then_inc(shift_ready, 1)
            link(nc.vector.tensor_tensor(crit, roots[:, 0:1], roots[:, 1:2], ALU.mult))
            link(nc.vector.tensor_scalar(crit, crit, 2.0 * SCALE, None, ALU.mult))
            link(nc.vector.scalar_tensor_tensor(crit, gstat[:, 2:3], 4.0, crit, ALU.mult, ALU.add))
            nc.vector.tensor_scalar(flag[:], crit[0:1, :], SPAN, None, ALU.is_le).then_inc(flag_ready, 1)

            def copy_sums(q, j):
                dve.wait_ge(values_added, (q + 1) * PAIR + (j + 1) * NT)
                dve.wait_ge(head_out[j], (q + 1) * STORED + 16)
                nc.vector.tensor_copy(osb[j][:], acc[j]).then_inc(acc_copied, 1)

            def dve_pair(nb, q, first):
                for x in range(PAIR):
                    if first and x in (0, BT):
                        dve.wait_ge(slab_in[x // BT], (nb + 1) * 16)
                    if not is_pool(x):
                        dve.wait_ge(scores_dve, q * ndve + dve_no(x) + 1)
                        slot_free(dve, q, x)
                        nc.vector.scalar_tensor_tensor(
                            ring[:, x % RING, :].rearrange("p (u c) -> p u c", u=2), s_dve[dve_no(x) % 2], SCALE / 2,
                            slab[:, x % NT, :].rearrange("p (u c) -> p u c", u=2), ALU.mult, ALU.add)\
                            .then_inc(biased, 1)
                    if x == 8:
                        copy_sums(q - 1, 1)
                    if x == NT + 8:
                        copy_sums(q, 0)

            dve.wait_ge(flag_ready, 1)
            narrow = dve.value_load(flag[0:1, 0:1], min_val=0, max_val=1)
            with dve.If(narrow == 1):
                dve.nop().then_inc(biased, 2)
                with dve.Fori(0, NBLK) as nb:
                    dve_pair(nb, nb * PAIRS, True)
                    with dve.Fori(1, PAIRS) as p:
                        dve_pair(nb, nb * PAIRS + p, False)
                copy_sums(NBLK * PAIRS - 1, 1)
            with dve.Else():
                dve.nop().then_inc(g_out_ready, 1)
                with dve.Fori(0, NT) as i:
                    with dve.Fori(0, HEADS) as h:
                        step = i * HEADS + h
                        dve.wait_ge(g_adj_in, (i + 1) * 16)
                        dve.wait_ge(g_scores, step + 1)
                        nc.vector.scalar_tensor_tensor(g_prob.rearrange("p (c n) -> p c n", n=CH), psum[:, :, 0:CH],
                                                       SCALE, g_adj.rearrange("p (c n) -> p c n", n=CH),
                                                       ALU.mult, ALU.add).then_inc(g_step, 1)
                        dve.wait_ge(g_step, step * 4 + 1)
                        nc.vector.tensor_tensor(g_prob, g_prob, g_adj, ALU.add).then_inc(g_step, 1)
                        dve.wait_ge(g_step, step * 4 + 2)
                        nc.vector.tensor_reduce(g_top, g_prob[:, 0:N], AX.X, ALU.max).then_inc(g_step, 1)
                        nc.vector.memset(g_prob[:, N:NP], 0.0).then_inc(g_step, 1)
                        dve.wait_ge(g_step, step * 4 + 4)
                        nc.vector.tensor_scalar(g_neg_max, g_top, -1.0, None, ALU.mult).then_inc(g_max, 1)
                        dve.wait_ge(g_summed, step + 2)
                        dve.wait_ge(g_stored, step * 16 + 16)
                        nc.vector.tensor_copy(osb[0][0:F + 1, 0:P], psum[0:F + 1, 7, 0:P]).then_inc(g_out_ready, 1)

            dve.nop().then_inc(x_row, 2)
            dve.nop().then_inc(y_ready, 2)
            dve.wait_ge(x_in2, 16)

            def divide(g, j):
                r = g * 2 + j
                dve.wait_ge(o_in[j], (g + 1) * 16)
                dve.wait_ge(y_ready, r + 1)
                nc.vector.reciprocal(recip_d[:, j, :], oblk[j][:, F * P:(F + 1) * P]).then_inc(recip_made, 1)
                dve.wait_ge(recip_made, r + 1)
                dve.wait_ge(y_turned, r + 1)
                nc.vector.tensor_tensor(yrow[j].rearrange("p (f c) -> p f c", f=F),
                                        oblk[j][:, 0:F * P].rearrange("p (f c) -> p f c", f=F),
                                        recip_d[:, j:j + 1, :].broadcast_to([P, F, P]), ALU.mult)\
                    .then_inc(y_ready, 1)

            def add_row(g, j):
                r = g * 2 + j
                dve.wait_ge(wo_done, r + 3)
                nc.vector.tensor_tensor(x_cur[:, bass.ds(r * P, P)], psum[:, 2 + j, 0:P],
                                        x_cur[:, bass.ds(r * P, P)], ALU.add).then_inc(x_row, 1)

            divide(0, 0)
            divide(0, 1)
            with dve.Fori(0, NT // 2 - 1) as g:
                for j in range(2):
                    divide(g + 1, j)
                    add_row(g, j)
            add_row(NT // 2 - 1, 0)
            add_row(NT // 2 - 1, 1)

            all8 = psum[:, :, 0:CH]

            def layernorm(n):
                dve.wait_ge(ln_mean, n + 1)
                nc.vector.tensor_tensor(chunks(ln_d), chunks(x_cur), all8, ALU.subtract).then_inc(ln_centered, 1)
                dve.wait_ge(ln_std, n + 1)
                nc.vector.reciprocal(ln_q[:], ln_q[:]).then_inc(ln_factor, 1)
                dve.wait_ge(ln_spread, n + 1)
                nc.vector.tensor_tensor(chunks(x_cur), chunks(ln_d), all8, ALU.mult).then_inc(ln_out, 1)

            dve.wait_ge(x_row, NT + 2)
            dve.nop().then_inc(x_ready, 1)
            layernorm(0)
            dve.wait_ge(ln_out, 1)
            dve.wait_ge(s_made, 1)
            nc.vector.tensor_scalar(chunks(a_row), all8, vecs[:, 2:3], None, ALU.add).then_inc(s1_copied, 1)
            dve.wait_ge(s2_copied, 1)
            link(nc.vector.tensor_reduce(s2_min, s2_row, AX.X, ALU.min))
            link(nc.vector.tensor_scalar(u_off, s2_min, 1.0, None, ALU.subtract))
            link(nc.vector.tensor_scalar(s2_row, s2_row, u_off, None, ALU.subtract))
            dve.wait_ge(h_copied, 1)
            link(nc.vector.tensor_reduce(h_sum, h_t[:, 0:N], AX.X, ALU.add))
            dve.wait_ge(nat_copied, 1)
            link(nc.vector.tensor_scalar(s2_pair[:, :, 1], s2_pair[:, :, 0], 0.2, None, ALU.mult))
            dve.nop().then_inc(u_done, 2)
            dve.nop().then_inc(deg_kept, 2)
            with dve.Fori(0, NT // 2) as g:
                for j in range(2):
                    r = g * 2 + j
                    dve.wait_ge(tile_in[j], (g + 1) * 16)
                    dve.wait_ge(u_done, r + 2)
                    nc.vector.scalar_tensor_tensor(work[0], tile_buf[j], 0.0, s2_row, ALU.is_gt, ALU.mult)\
                        .then_inc(neighbour_step, 1)
                    dve.wait_ge(neighbour_step, r * 2 + 1)
                    nc.vector.tensor_reduce(u_now[:, j:j + 1], work[0], AX.X, ALU.max).then_inc(neighbour_step, 1)
                    dve.wait_ge(neighbour_step, r * 2 + 2)
                    nc.vector.tensor_tensor(u_nat[:, bass.ds(r, 1)], u_now[:, j:j + 1], zero_col[:], ALU.add)\
                        .then_inc(u_done, 1)
                    dve.wait_ge(deg_done, r + 3)
                    nc.vector.tensor_tensor(deg_nat[:, bass.ds(r, 1)], deg_now[j][:], zero_col[:], ALU.add)\
                        .then_inc(deg_kept, 1)
            dve.wait_ge(deg_kept, NT + 2)
            dve.wait_ge(u_done, NT + 2)
            by_tile = lambda ap: ap.rearrange("p (k c) -> p k c", c=P)
            ident_all = ident[:].rearrange("p (o c) -> p o c", o=1).broadcast_to([P, NT, P])

            def spread(col):
                nc.vector.tensor_tensor(by_tile(work[0]), ident_all,
                                        col[:].rearrange("p (k o) -> p k o", o=1).broadcast_to([P, NT, P]),
                                        ALU.mult).then_inc(spread_in, 1)

            spread(u_nat)
            dve.wait_ge(spread_out, 1)
            nc.vector.tensor_scalar(chunks(none_row), all8, 0.0, None, ALU.is_equal)
            link(nc.vector.scalar_tensor_tensor(chunks(work[1]), all8, u_off, chunks(a_row), ALU.add, ALU.add))
            link(nc.vector.scalar_tensor_tensor(work[2], work[1], 0.2, work[1], ALU.mult, ALU.max))
            link(nc.vector.scalar_tensor_tensor(b_row, a_row, 0.2, work[2], ALU.mult, ALU.subtract))
            link(nc.vector.tensor_tensor(a_row, a_row, work[2], ALU.subtract))
            link(nc.vector.tensor_scalar(u_nat[:], deg_nat[:], 0.0, None, ALU.is_equal))
            link(nc.vector.tensor_tensor(deg_nat[:], deg_nat[:], u_nat[:], ALU.add))
            link(nc.vector.reciprocal(deg_nat[:], deg_nat[:]))
            spread(deg_nat)
            dve.wait_ge(spread_out, 2)
            link(nc.vector.tensor_copy(chunks(recip_deg), all8))
            for ap in (a_row, b_row, s2_pair[:]):
                link(nc.vector.tensor_scalar(ap, ap, 1.0 / MASK, None, ALU.mult))
            dve.nop().then_inc(exponent_ready, 4)
            dve.nop().then_inc(spread_in, 1)
            for half in range(2):
                cut = slice(half * HN, (half + 1) * HN)
                def exponents(g, i):
                    j, k = i % 2, g * 4 + i
                    r = half * NT + k
                    low, t_now = work[j][:, HN:2 * HN], work[j][:, 0:HN]
                    dve.wait_ge(gat_added, r + 1)
                    nc.vector.tensor_tensor(stat_k[j][:], h_nat[:, bass.ds(k * P, P)],
                                            h_nat[:, bass.ds(k * P, P)], ALU.max).then_inc(gat_step, 1)
                    dve.wait_ge(exponent_ready, r + 3)
                    nc.vector.tensor_tensor(s2_now[j][:].rearrange("p (o c) -> p o c", o=1),
                                            s2_pair[:, bass.ds(k, 1), :], s2_pair[:, bass.ds(k, 1), :],
                                            ALU.max).then_inc(gat_step, 1)
                    dve.wait_ge(gat_step, r * 4 + 2)
                    nc.vector.tensor_scalar(low, b_row[:, cut], s2_now[j][:, 1:2], None, ALU.add)\
                        .then_inc(gat_step, 1)
                    dve.wait_ge(gat_step, r * 4 + 3)
                    nc.vector.scalar_tensor_tensor(t_now, a_row[:, cut], s2_now[j][:, 0:1], low,
                                                   ALU.add, ALU.max).then_inc(gat_step, 1)
                    dve.wait_ge(gat_step, r * 4 + 4)
                    dve.wait_ge(half_in[i], loads_of(half, g, i) * 16)
                    nc.vector.scalar_tensor_tensor(t_now, half_buf[i], 0.0, t_now,
                                                   ALU.is_le, ALU.subtract).then_inc(exponent_ready, 1)

                for_tiles(dve, exponents)
                dve.wait_ge(den_made, half + 1)
                link(nc.vector.tensor_scalar(den_sb[:], psum[:, 4, 0:CH], 0.0, float(N), ALU.is_equal, ALU.mult))
                link(nc.vector.tensor_tensor(den_sb[:], den_sb[:], psum[:, 4, 0:CH], ALU.add))
                nc.vector.reciprocal(den_sb[:], den_sb[:]).then_inc(den_copied, 1)
                half4 = lambda ap: ap.rearrange("p (c n) -> p c n", n=CH)
                link(nc.vector.scalar_tensor_tensor(half4(work[0][:, 0:HN]), half4(none_row[:, cut]), h_sum,
                                                    psum[:, 0:4, 0:CH], ALU.mult, ALU.add))
                dve.wait_ge(den_spread, half + 1)
                link(nc.vector.tensor_tensor(half4(work[0][:, 0:HN]), half4(work[0][:, 0:HN]),
                                             psum[:, 4:8, 0:CH], ALU.mult))
                last = nc.vector.tensor_tensor(x_cur[:, cut], x_cur[:, cut], work[0][:, 0:HN], ALU.add)
                link(last)
                dve.nop().then_inc(half_done, 1)
            dve.nop().then_inc(x_ready, 1)
            layernorm(1)
            for n in range(2):
                dve.wait_ge(ln_out, n + 2)
                dve.wait_ge(nat_copied, n + 2)
                with dve.Fori(0, NT // 2) as g:
                    for j in range(2):
                        dve.wait_ge(sweep_added, n * NT + g * 2 + j + 3)
                        k = g * 2 + j
                        nc.vector.tensor_tensor(stat_k[j][:], x_nat[:, bass.ds(k * P, P)],
                                                x_nat[:, bass.ds(k * P, P)], ALU.max).then_inc(stat_ready, 1)
                if n == 0:
                    dve.wait_ge(sweep_done, 1)
                    nc.vector.tensor_tensor(chunks(work[0]), all8, chunks(recip_deg), ALU.mult).then_inc(sum_copied, 1)
                    nc.vector.tensor_tensor(bn_bias, vecs[:, 3:4], vecs[:, 4:5], ALU.add).then_inc(sum_copied, 1)
                    dve.wait_ge(dense_copied, 1)
                    link(nc.vector.tensor_reduce(bn_mean, work[1][:, 0:N], AX.X, ALU.add))
                    link(nc.vector.tensor_scalar(bn_mean, bn_mean, 1.0 / N, None, ALU.mult))
                    nc.vector.tensor_scalar(work[2], work[1], bn_mean, None, ALU.subtract).then_inc(bn_centered, 1)
                    dve.wait_ge(bn_squared, 2)
                    link(nc.vector.reciprocal(bn_std, bn_std))
                    nc.vector.tensor_tensor(bn_gain, bn_std, vecs[:, 5:6], ALU.mult).then_inc(bn_ready, 1)
                    dve.wait_ge(bn_out, 1)
                    nc.vector.tensor_tensor(x_cur, x_cur, work[0], ALU.add).then_inc(x_ready, 1)
                else:
                    dve.wait_ge(dense_made, 2)
                    nc.vector.scalar_tensor_tensor(chunks(x_cur), all8, vecs[:, 7:8], chunks(x_cur),
                                                   ALU.add, ALU.add).then_inc(x_ready, 1)
                layernorm(n + 2)


def kernel(**inputs):
    import numpy as np
    import concourse.bacc as bacc
    from concourse import mybir
    from concourse.bass_utils import run_bass_kernel_spmd

    n, padded, p = 3327, 3328, 128
    a = {k: np.asarray(v) for k, v in inputs.items()}
    lay = {}
    lay["xT"] = np.zeros((p, padded), a["x"].dtype)
    lay["xT"][:, :n] = a["x"].T
    lay["adjN"] = np.zeros((padded, padded), a["adj"].dtype)
    lay["adjN"][:n, :n] = a["adj"]
    lay["adjT"] = lay["adjN"].T
    for k in ("Wq", "Wk", "Wv"):
        lay[k] = a["L0_gnn_" + k].reshape(p, 8, p).transpose(2, 1, 0).reshape(p, 8 * p)
    lay["Wo"] = a["L0_gnn_Wo"].reshape(p, p, 8).transpose(1, 2, 0)
    w3 = a["L3_gnn_W"]
    mats = [a["L1_gnn_W"], a["L2_gnn_W_n"].T, a["L2_gnn_W_c"].T, w3[:, p:].T, w3[:, :p].T]
    lay["mats"] = np.stack(mats, axis=1)
    vecs = [a["L1_gnn_a1"], a["L1_gnn_a2"], np.broadcast_to(a["L1_gnn_a_bias"], (p,)), a["L2_gnn_b_n"],
            a["L2_gnn_b_c"], a["L2_gnn_gamma"], a["L2_gnn_beta"], a["L3_gnn_b"]]
    lay["vecs"] = np.stack(vecs, axis=1)
    nc = bacc.Bacc("TRN2", target_bir_lowering=False, num_devices=1)
    arrays, t = {}, {}
    for k, v in lay.items():
        arrays["in_" + k] = np.ascontiguousarray(v)
        t[k] = nc.dram_tensor("in_" + k, v.shape, mybir.dt.from_np(v.dtype), kind="ExternalInput").ap()
    out = nc.dram_tensor("out_T", (p, n), mybir.dt.float32, kind="ExternalOutput").ap()
    build(nc, t, out)
    got = run_bass_kernel_spmd(nc, [arrays], core_ids=[0])
    return np.ascontiguousarray(got.results[0]["out_T"].T)
```
